# Optimizing a Trainium2 kernel written in Bass

```python
import numpy as np
import jax
import jax.numpy as jnp

def _softmax(x, axis=-1):
    return jax.nn.softmax(x, axis=axis)

def _gelu(x):
    return jax.nn.gelu(x, approximate=True)

def _silu(x):
    return jax.nn.silu(x)

def _sigmoid(x):
    return jax.nn.sigmoid(x)

def _layernorm(x, axis=-1, eps=1e-05):
    m = jnp.mean(x, axis=axis, keepdims=True)
    v = jnp.var(x, axis=axis, keepdims=True)
    return (x - m) / jnp.sqrt(v + eps)

def _scatter_add(tgt, idx, src, axis=0):
    return tgt.at[idx].add(src)

def _segment_sum(src, seg, n):
    return jax.ops.segment_sum(src, seg, n)
kernel_name = 'mk_lm_tower_d1_tok_ids512_r4_9d927a'

def setup_inputs(seed: int=0):
    np.random.seed(seed)
    _w = jnp.asarray

    def _rec_inputs():
        import jax
        import jax.numpy as jnp
        _rk = jax.random.key(seed)
        x = jax.random.randint(jax.random.fold_in(_rk, 1), (2, 2048), 0, 64, jnp.int32)
        return x
    x = _rec_inputs()

    def _L0_tok_setup():
        import jax, jax.numpy as jnp
        import numpy as np
        key = jax.random.key(seed)
        k1, k2 = jax.random.split(key)
        N_SYMBOLS, D = (64, 128)
        B, T = (64, 256)
        val = np.sqrt(3.0) * np.sqrt(2.0 / (N_SYMBOLS + D))
        weight = jax.random.uniform(k1, (N_SYMBOLS, D), jnp.float32, -val, val)
        x = jax.random.randint(k2, (B, T), 0, N_SYMBOLS, dtype=jnp.int64)
        end_ids = jnp.arange(2, dtype=jnp.int64)
        return {'weight': weight, 'x': x, 'end_ids': end_ids}
    _L0_tok_all = _L0_tok_setup()
    _L0_tok_in = {k: v for k, v in _L0_tok_all.items() if k in ('weight', 'end_ids')}
    del _L0_tok_all

    def _L0_attn_setup():
        import jax, jax.numpy as jnp
        import numpy as np
        EPS = 1e-05

        def _layernorm(x):
            mu = x.mean(axis=-1, keepdims=True)
            var = x.var(axis=-1, keepdims=True)
            return (x - mu) / jnp.sqrt(var + EPS)
        key = jax.random.key(seed)
        k1, k2, k3, k4, k5 = jax.random.split(key, 5)
        B, T, E, H = (8, 512, 128, 8)
        d = E // H
        return {'input1': jax.random.normal(k1, (B, T, E), dtype=jnp.float32), 'Wq': jax.random.normal(k2, (H, d), dtype=jnp.float32) * 0.1, 'Wk': jax.random.normal(k3, (H, d), dtype=jnp.float32) * 0.1, 'Wv': jax.random.normal(k4, (H, d, d), dtype=jnp.float32) * 0.1, 'Wm': jax.random.normal(k5, (E, E), dtype=jnp.float32) * 0.05}
    _L0_attn_all = _L0_attn_setup()
    _L0_attn_in = {k: v for k, v in _L0_attn_all.items() if k in ('Wq', 'Wk', 'Wv', 'Wm')}
    del _L0_attn_all

    def _L0_ffn_setup():
        import jax, jax.numpy as jnp
        import numpy as np
        D = 128
        E = 8
        K = 2
        EXP = 4
        LN_EPS = 1e-05
        key = jax.random.key(seed)
        ks = jax.random.split(key, 8)
        B, T = (8, 512)
        Dh = D * EXP
        x = jax.random.normal(ks[0], (B, T, D), dtype=jnp.float32)
        ln_g = jnp.ones((D,), dtype=jnp.float32)
        ln_b = jnp.zeros((D,), dtype=jnp.float32)
        lim_r = np.sqrt(6.0 / (D + E)).astype(np.float32)
        w_r = jax.random.uniform(ks[1], (E, D), dtype=jnp.float32, minval=-lim_r, maxval=lim_r)
        b_r = jnp.zeros((E,), dtype=jnp.float32)
        lim1 = np.sqrt(6.0 / (D + Dh)).astype(np.float32)
        W1 = jax.random.uniform(ks[2], (E, D, Dh), dtype=jnp.float32, minval=-lim1, maxval=lim1)
        b1 = jnp.zeros((E, Dh), dtype=jnp.float32)
        W2 = jax.random.uniform(ks[3], (E, Dh, D), dtype=jnp.float32, minval=-lim1, maxval=lim1)
        b2 = jnp.zeros((E, D), dtype=jnp.float32)
        return {'x': x, 'ln_g': ln_g, 'ln_b': ln_b, 'w_r': w_r, 'b_r': b_r, 'W1': W1, 'b1': b1, 'W2': W2, 'b2': b2}
    _L0_ffn_all = _L0_ffn_setup()
    _L0_ffn_in = {k: v for k, v in _L0_ffn_all.items() if k in ('ln_g', 'ln_b', 'w_r', 'b_r', 'W1', 'b1', 'W2', 'b2')}
    del _L0_ffn_all
    return {'x': x, 'L0_tok_weight': _L0_tok_in['weight'], 'L0_tok_end_ids': _L0_tok_in['end_ids'], 'L0_attn_Wq': _L0_attn_in['Wq'], 'L0_attn_Wk': _L0_attn_in['Wk'], 'L0_attn_Wv': _L0_attn_in['Wv'], 'L0_attn_Wm': _L0_attn_in['Wm'], 'L0_ffn_ln_g': _L0_ffn_in['ln_g'], 'L0_ffn_ln_b': _L0_ffn_in['ln_b'], 'L0_ffn_w_r': _L0_ffn_in['w_r'], 'L0_ffn_b_r': _L0_ffn_in['b_r'], 'L0_ffn_W1': _L0_ffn_in['W1'], 'L0_ffn_b1': _L0_ffn_in['b1'], 'L0_ffn_W2': _L0_ffn_in['W2'], 'L0_ffn_b2': _L0_ffn_in['b2']}

def reference(x, L0_tok_weight, L0_tok_end_ids, L0_attn_Wq, L0_attn_Wk, L0_attn_Wv, L0_attn_Wm, L0_ffn_ln_g, L0_ffn_ln_b, L0_ffn_w_r, L0_ffn_b_r, L0_ffn_W1, L0_ffn_b1, L0_ffn_W2, L0_ffn_b2):
    import jax
    import jax.numpy as jnp

    def _L0_tok_ref(weight, x, end_ids):
        import jax, jax.numpy as jnp
        import numpy as np
        emb = weight[x]
        end_vecs = weight[end_ids] * jnp.asarray(1.5, weight.dtype)
        B, T, D = emb.shape

        def step(carry, inp):
            vec, has = carry
            e_t, x_t = inp
            eq = x_t[:, None] == end_ids[None, :]
            is_end = eq.any(axis=1)
            idx = jnp.argmax(eq, axis=1)
            out = e_t + jnp.where((has & ~is_end)[:, None], vec, jnp.zeros((), e_t.dtype))
            new_vec = jnp.where(is_end[:, None], end_vecs[idx], vec)
            new_has = has | is_end
            return ((new_vec, new_has), out)
        init = (jnp.zeros((B, D), emb.dtype), jnp.zeros((B,), dtype=bool))
        _, outs = jax.lax.scan(step, init, (emb.transpose(1, 0, 2), x.T), reverse=True)
        return outs.transpose(1, 0, 2)

    def _L0_attn_ref(input1, Wq, Wk, Wv, Wm):
        import jax, jax.numpy as jnp
        import numpy as np
        EPS = 1e-05

        def _layernorm(x):
            mu = x.mean(axis=-1, keepdims=True)
            var = x.var(axis=-1, keepdims=True)
            return (x - mu) / jnp.sqrt(var + EPS)
        B, T, E = input1.shape
        H, d = Wq.shape
        xn = _layernorm(input1)
        xh = xn.reshape(B, T, H, d)
        Q = jnp.einsum('bthd,hd->bht', xh, Wq)
        K = jnp.einsum('bthd,hd->bht', xh, Wk)
        V = jnp.einsum('bthd,hde->bhte', xh, Wv)
        A = -(Q[:, :, :, None] - K[:, :, None, :]) ** 2
        P = jax.nn.softmax(A / d ** 0.5, axis=-1)
        O = jnp.einsum('bhts,bhse->bhte', P, V)
        head_result = O.transpose(0, 2, 1, 3).reshape(B, T, E)
        return head_result @ Wm + input1

    def _L0_ffn_ref(x, ln_g, ln_b, w_r, b_r, W1, b1, W2, b2):
        import jax, jax.numpy as jnp
        import numpy as np
        D = 128
        E = 8
        K = 2
        EXP = 4
        LN_EPS = 1e-05
        B, T, d = x.shape
        mu = jnp.mean(x, axis=-1, keepdims=True)
        var = jnp.mean(jnp.square(x - mu), axis=-1, keepdims=True)
        h = (x - mu) * jax.lax.rsqrt(var + LN_EPS) * ln_g + ln_b
        logits = jnp.einsum('btd,ed->bte', h, w_r) + b_r
        topk_vals, topk_idx = jax.lax.top_k(logits, K)
        gates = jax.nn.softmax(topk_vals, axis=-1)
        hf = h.reshape(B * T, d)
        hid = jax.nn.gelu(jnp.einsum('nd,edf->nef', hf, W1) + b1, approximate=False)
        expert_stack = jnp.einsum('nef,efd->ned', hid, W2) + b2
        idx_flat = topk_idx.reshape(B * T, K)
        gates_flat = gates.reshape(B * T, K)
        gathered = jnp.take_along_axis(expert_stack, idx_flat[:, :, None], axis=1)
        mixed = jnp.sum(gathered * gates_flat[:, :, None], axis=1).reshape(B, T, d)
        return x + mixed
    h = _L0_tok_ref(L0_tok_weight, x, L0_tok_end_ids)
    h = h + _L0_attn_ref(_layernorm(h, axis=-1), L0_attn_Wq, L0_attn_Wk, L0_attn_Wv, L0_attn_Wm)
    h = h + _L0_ffn_ref(_layernorm(h, axis=-1), L0_ffn_ln_g, L0_ffn_ln_b, L0_ffn_w_r, L0_ffn_b_r, L0_ffn_W1, L0_ffn_b1, L0_ffn_W2, L0_ffn_b2)
    return h

_drawn_inputs = setup_inputs


def setup_inputs(seed=0):
    import zlib

    import numpy as np

    out = dict(_drawn_inputs(seed))
    spreads = {'L0_ffn_ln_g': (1.0, 0.2),
     'L0_ffn_ln_b': (0.0, 0.1),
     'L0_ffn_b_r': (0.0, 0.359),
     'L0_ffn_b1': (0.0, 0.294),
     'L0_ffn_b2': (0.0, 0.1)}
    factors = {'L0_attn_Wq': 5.748, 'L0_attn_Wk': 6.091}
    for name, (base, spread) in spreads.items():
        noise = np.random.default_rng([zlib.crc32(name.encode()), seed]).standard_normal(out[name].shape)
        drawn = base * np.exp(spread * noise) if base else spread * noise
        out[name] = jnp.asarray(drawn.astype(out[name].dtype))
    for name, factor in factors.items():
        out[name] = (out[name] * factor).astype(out[name].dtype)
    return out
```

```python
from contextlib import ExitStack

import numpy as np

import concourse.bass as bass
from concourse import mybir

F32 = mybir.dt.float32
F32R = mybir.dt.float32r
BF16 = mybir.dt.bfloat16
I32 = mybir.dt.int32
ALU = mybir.AluOpType
ACT = mybir.ActivationFunctionType
AX = mybir.AxisListType

P = 128
B, T, D = 2, 2048, 128
SYM = 64
STATES = 3
CLS = STATES * SYM
ROWS = B * CLS
NT = ROWS // P
H, HD = 8, 16
HA = HD + 1
E, DH = 8, 512
FT = DH // P
J = T // P
EPS = 1e-5
HALF = 64
PAIRS = H // 2
ABSENT = 1e18
BANK = 512


def build(nc, x, weight, end_ids, wq, wk, wv, wm, ln_g, ln_b, w_r, b_r, w1, b1, w2, b2, out):
    ctx = ExitStack()
    with ctx:
        def sb(name, shape, dt=F32):
            return ctx.enter_context(nc.sbuf_tensor(name, shape, dt))

        def sem(name):
            return ctx.enter_context(nc.semaphore(name))

        ps = ctx.enter_context(nc.psum_tensor("ps", [P, 8, BANK], F32))

        x_i = sb("x_i", [P, B, J], I32)
        ends_i = sb("ends_i", [P, 2], I32)
        emb = sb("emb", [SYM, D])
        wq_col = sb("wq_col", [P, 1])
        wk_col = sb("wk_col", [P, 1])
        wv_diag = sb("wv_diag", [P, D])
        wm_sb = sb("wm_sb", [P, D])
        g_col = sb("g_col", [P, 1])
        b_col = sb("b_col", [P, 1])
        wr_t = sb("wr_t", [P, E])
        br_row = sb("br_row", [P, E])
        b1_col = sb("b1_col", [P, E, FT])
        b2_sb = sb("b2_sb", [E, D])
        w1_f = sb("w1_f", [P, E, DH])
        w2_f = w1_f[:].rearrange("p e (t d) -> p e t d", t=FT)
        w1_hi = sb("w1_hi", [P, E, DH], F32R)
        w1_lo = sb("w1_lo", [P, E, DH], F32R)
        w2_hi = sb("w2_hi", [P, E, FT, D], F32R)
        w2_lo = sb("w2_lo", [P, E, FT, D], F32R)

        ident = sb("ident", [P, P])
        iota_sym = sb("iota_sym", [P, SYM])
        iota_part = sb("iota_part", [P, 1])
        iota_code = sb("iota_code", [P, B * STATES])
        hot_id = sb("hot_id", [P, NT])
        head_mask = sb("head_mask", [P, H])
        ident_b = sb("ident_b", [B * J, B * J], BF16)
        batch_sel = sb("batch_sel", [B * STATES, NT, P], BF16)
        state_absent = sb("state_absent", [B * STATES, STATES])
        before = sb("before", [P, E, E])
        neg_half = sb("neg_half", [P, NT])

        x_f = sb("x_f", [P, B, J])
        ends_f = sb("ends_f", [P, 2])
        code0 = sb("code0", [P, B, J])
        code = sb("code", [P, B, J])
        no_end = sb("no_end", [P, B, J])
        local = sb("local", [P, B, J])
        state = sb("state", [P, B, J])
        cls = sb("cls", [P, B, J])
        hot_code = sb("hot_code", [P, B * J, B * STATES], BF16)
        total_row = sb("total_row", [B, P])
        total_none = sb("total_none", [B, P])
        carry_row = sb("carry_row", [B, P + 1])
        carry = sb("carry", [P, B])
        count_row = sb("count_row", [B * STATES, SYM])
        is_absent = sb("is_absent", [B * STATES, SYM])
        penalty = sb("penalty", [B * STATES, STATES, SYM], BF16)
        count = sb("count", [P, B * STATES])
        cls_row = sb("cls_row", [B * J, P], BF16)
        hot = sb("hot", [P, NT, J, P], F32R)

        end_hot = sb("end_hot", [SYM, 2])
        gather = sb("gather", [SYM, B, STATES, SYM])
        h0 = sb("h0", [P, NT, D])
        stats = sb("stats", [P, NT, 6])
        mv = sb("mv", [P, NT, 2])
        var = sb("var", [P, NT])
        rstd = sb("rstd", [P, NT])
        u = sb("u", [P, NT, D])
        stats2 = sb("stats2", [P, NT, 6])
        mv2 = sb("mv2", [P, NT, 2])
        var2 = sb("var2", [P, NT])
        rstd2 = sb("rstd2", [P, NT])
        xn = sb("xn", [P, NT, D])
        xn_t = sb("xn_t", [P, ROWS])
        q_cols = sb("q_cols", [P, H])
        k_cols = sb("k_cols", [P, H])
        k_rep = sb("k_rep", [P, H, P])
        ones_rep = sb("ones_rep", [P, P])
        neg_q = sb("neg_q", [P, NT, H])
        v_aug = sb("v_aug", [P, STATES, PAIRS, 2, HA])
        v_cnt = sb("v_cnt", [P, B, STATES, PAIRS, 2, HA])
        dist = sb("dist", [P, NT, STATES, H, SYM])
        near = sb("near", [P, NT, H])
        prob = dist
        prob_t = sb("prob_t", [P, 2, STATES, PAIRS, P])
        hot_sym = prob_t[:, 1, 0:2].rearrange("p s k q -> p (s k q)").bitcast(BF16).rearrange("p (t c) -> p t c", c=SYM)
        rden = sb("rden", [P, NT, H])
        heads = sb("heads", [P, NT, H, HD])
        heads_t = sb("heads_t", [P, NT, P])
        h1 = sb("h1", [P, NT, D])
        stats3 = sb("stats3", [P, NT, 6])
        mv3 = sb("mv3", [P, NT, 2])
        var3 = sb("var3", [P, NT])
        rstd3 = sb("rstd3", [P, NT])
        w_ln = sb("w_ln", [P, NT, D])
        stats4 = sb("stats4", [P, NT, 6])
        mv4 = sb("mv4", [P, NT, 2])
        var4 = sb("var4", [P, NT])
        rstd4 = sb("rstd4", [P, NT])
        hn = sb("hn", [P, NT, D])
        hn_t = sb("hn_t", [P, ROWS])
        hn_hi = sb("hn_hi", [P, ROWS], F32R)
        hn_lo = sb("hn_lo", [P, ROWS], F32R)

        logit = sb("logit", [P, NT, E])
        above = sb("above", [P, NT, E, E])
        tie = sb("tie", [P, NT, E, E])
        rank = sb("rank", [P, NT, E])
        top = sb("top", [P, NT, 1])
        shifted = sb("shifted", [P, NT, E])
        e_exp = sb("e_exp", [P, NT, E])
        chosen = sb("chosen", [P, NT, E])
        gsum = sb("gsum", [P, NT, 1])
        grec = sb("grec", [P, NT, 1])
        gate = sb("gate", [P, NT, E])
        gate_t = sb("gate_t", [E, NT, P])

        hid = dist[:].rearrange("p t s h c -> p (t s h c)")[:, 0:2 * FT * ROWS].rearrange("p (b f r) -> p b f r", b=2, f=FT)
        hid_hi = sb("hid_hi", [P, 2, FT, ROWS], F32R)
        hid_lo = sb("hid_lo", [P, 2, FT, ROWS], F32R)
        acc = sb("acc", [P, NT, D])
        tab_hi = sb("tab_hi", [P, NT, D], F32R)
        tab_lo = sb("tab_lo", [P, NT, D], F32R)
        y = w1_f[:].rearrange("p e (j d) -> p (e j) d", d=D).rearrange("p (b j) d -> p b j d", b=B)

        x_in = sem("x_in")
        end_in = sem("end_in")
        emb_in = sem("emb_in")
        small_in = sem("small_in")
        w1_in = [sem(f"w1_in{i}") for i in range(4)]
        w2_in = [sem(f"w2_in{e}") for e in range(E)]
        y_out = sem("y_out")
        pool_step = sem("pool_step")
        consts_ready = sem("consts_ready")
        diag_zero = sem("diag_zero")
        ident_ready = sem("ident_ready")
        gather_ready = sem("gather_ready")
        aug_ready = sem("aug_ready")
        h0_done = sem("h0_done")
        var_ready = sem("var_ready")
        rstd_ready = sem("rstd_ready")
        xn_ready = sem("xn_ready")
        xnt_done = sem("xnt_done")
        xnt_ready = sem("xnt_ready")
        wqk_ready = sem("wqk_ready")
        krep_ready = sem("krep_ready")
        qv_done = sem("qv_done")
        negq_ready = sem("negq_ready")
        total_ready = sem("total_ready")
        total_done = sem("total_done")
        carry_ready = sem("carry_ready")
        carry_done = sem("carry_done")
        hot_ready = sem("hot_ready")
        countrow_done = sem("countrow_done")
        countrow_ready = sem("countrow_ready")
        penalty_ready = sem("penalty_ready")
        count_done = sem("count_done")
        cls_ready = sem("cls_ready")
        clsrow_done = sem("clsrow_done")
        clsrow_ready = sem("clsrow_ready")
        v_ready = sem("v_ready")
        kb_done = sem("kb_done")
        dist_ready = sem("dist_ready")
        shift_ready = sem("shift_ready")
        prob_ready = sem("prob_ready")
        pt_done = sem("pt_done")
        pt_act = sem("pt_act")
        pt_dve = sem("pt_dve")
        o_done = sem("o_done")
        heads_ready = sem("heads_ready")
        headst_done = sem("headst_done")
        headst_ready = sem("headst_ready")
        att_done = sem("att_done")
        att_read = sem("att_read")
        hn_ready = sem("hn_ready")
        hnt_done = sem("hnt_done")
        hnt_ready = sem("hnt_ready")
        split_ready = sem("split_ready")
        logit_done = sem("logit_done")
        logit_read = sem("logit_read")
        shifted_ready = sem("shifted_ready")
        gexp_ready = sem("gexp_ready")
        gate_ready = sem("gate_ready")
        gatet_done = sem("gatet_done")
        gatet_ready = sem("gatet_ready")
        w1_split = sem("w1_split")
        w2_hi_ready = sem("w2_hi_ready")
        w2_lo_ready = sem("w2_lo_ready")
        up_done = sem("up_done")
        gelu_ready = sem("gelu_ready")
        hi_ready = sem("hi_ready")
        lo_ready = sem("lo_ready")
        down_done = sem("down_done")
        down_read = sem("down_read")
        bc_done = sem("bc_done")
        hot_out = sem("hot_out")
        bias_done = sem("bias_done")
        table_ready = sem("table_ready")
        y_done = sem("y_done")
        y_act = sem("y_act")
        y_dve = sem("y_dve")
        dve_step = sem("dve_step")

        BK_H0, BK_XNT, BK_QV, BK_CNT, BK_CHAIN, BK_PT, BK_O = 4, 5, 6, 7, 3, 4, 7
        KB = 3
        QCOL = STATES * D
        UNITS = NT * H // 2
        HOT_STEPS = NT * J // 4
        Y_GROUPS = B * J // 4
        SMALL = 9 + H

        block = ctx.enter_context(nc.Block())

        @block.sync
        def _(sp):
            sp.dma_start(x_i[:], x.rearrange("b (p j) -> p b j", p=P)).then_inc(x_in, 16)
            sp.dma_start(emb[:], weight).then_inc(emb_in, 16)
            for dst, src in ((wm_sb[:], wm), (g_col[:], ln_g), (b_col[:], ln_b), (wr_t[:], w_r),
                             (br_row[:], b_r.to_broadcast([P, E])), (b2_sb[:], b2),
                             (b1_col[:], b1)):
                sp.dma_start(dst, src).then_inc(small_in, 16)
            for i in range(4):
                sp.dma_start(w1_f[:, 2 * i:2 * i + 2, :],
                             w1[2 * i:2 * i + 2].rearrange("e d f -> d e f")).then_inc(w1_in[i], 16)
            for e in range(E):
                sp.wait_ge(w1_split, 2 * (e + 1))
                sp.dma_start(w2_f[:, e], w2[e].rearrange("(t f) d -> f t d", f=P)).then_inc(w2_in[e], 16)
            for g in range(0, Y_GROUPS, 2):
                b, j = g * 4 // J, g * 4 % J
                sp.wait_ge(y_act, g // 2 + 1)
                sp.wait_ge(y_dve, g // 2 + 1)
                sp.dma_start(out[b].rearrange("(p j) d -> p j d", j=J)[:, j:j + 8, :],
                             y[:, b, j:j + 8, :]).then_inc(y_out, 16)
            sp.wait_ge(y_out, 16 * Y_GROUPS // 2)

        @block.gpsimd
        def _(pool):
            n = 0

            def step(ins):
                nonlocal n
                n += 1
                ins.then_inc(pool_step, 1)

            def settle():
                pool.wait_ge(pool_step, n)

            nc.gpsimd.memset(wv_diag[:], 0.0).then_inc(diag_zero, 1)
            step(nc.gpsimd.memset(ident[:], 0.0))
            step(nc.gpsimd.memset(head_mask[:], 1.0))
            step(nc.gpsimd.memset(before[:], 1.0))
            step(nc.gpsimd.memset(state_absent[:], 0.0))
            step(nc.gpsimd.memset(neg_half[:], -0.5))
            step(nc.gpsimd.memset(ones_rep[:], 1.0))
            step(nc.gpsimd.memset(batch_sel[:], 1.0))
            settle()
            step(nc.gpsimd.affine_select(out=ident[:], in_=ident[:], compare_op=ALU.not_equal, fill=1.0,
                                         base=0, pattern=[[-1, P]], channel_multiplier=1))
            step(nc.gpsimd.affine_select(out=head_mask[:], in_=head_mask[:], compare_op=ALU.is_ge, fill=0.0,
                                         base=0, pattern=[[-HD, H]], channel_multiplier=1))
            step(nc.gpsimd.affine_select(out=before[:], in_=before[:], compare_op=ALU.is_gt, fill=0.0,
                                         base=0, pattern=[[1, E], [-1, E]], channel_multiplier=0))
            settle()
            step(nc.gpsimd.affine_select(out=head_mask[:], in_=head_mask[:], compare_op=ALU.is_ge, fill=0.0,
                                         base=HD - 1, pattern=[[HD, H]], channel_multiplier=-1))
            nc.gpsimd.iota(iota_sym[:], pattern=[[1, SYM]], base=0, channel_multiplier=0,
                           allow_small_or_imprecise_dtypes=True).then_inc(consts_ready, 1)
            nc.gpsimd.iota(iota_part[:], pattern=[[0, 1]], base=0, channel_multiplier=1,
                           allow_small_or_imprecise_dtypes=True).then_inc(consts_ready, 1)
            nc.gpsimd.iota(iota_code[:], pattern=[[1, B * STATES]], base=0, channel_multiplier=0,
                           allow_small_or_imprecise_dtypes=True).then_inc(consts_ready, 1)
            for k, (v, r) in enumerate(((var, rstd), (var2, rstd2))):
                pool.wait_ge(var_ready, k + 1)
                nc.gpsimd.tensor_tensor(r[:], v[:], neg_half[:], ALU.pow).then_inc(rstd_ready, 1)
            nc.gpsimd.memset(v_aug[:], 0.0).then_inc(aug_ready, 1)
            flat = batch_sel[:].rearrange("k t p -> k (t p)").rearrange("k (b c) -> k b c", b=B)
            step(nc.gpsimd.affine_select(out=flat[:, 0:1], in_=flat[:, 0:1], compare_op=ALU.is_ge, fill=0.0,
                                         base=STATES - 1, pattern=[[0, 1], [0, CLS]], channel_multiplier=-1))
            step(nc.gpsimd.affine_select(out=flat[:, 1:2], in_=flat[:, 1:2], compare_op=ALU.is_ge, fill=0.0,
                                         base=-STATES, pattern=[[0, 1], [0, CLS]], channel_multiplier=1))
            for b in range(B):
                step(nc.gpsimd.affine_select(out=state_absent[:], in_=state_absent[:],
                                             compare_op=ALU.not_equal, fill=ABSENT,
                                             base=-STATES * b, pattern=[[-1, STATES]], channel_multiplier=1))
                settle()
            def split_w1(e):
                pool.wait_ge(w1_in[e // 2], 16)
                nc.gpsimd.tensor_scalar(w1_hi[:, e], w1_f[:, e], 1.0, 0.0, ALU.mult, ALU.add).then_inc(w1_split, 1)
                pool.wait_ge(w1_split, 2 * e + 1)
                nc.gpsimd.tensor_tensor(w1_lo[:, e], w1_f[:, e], w1_hi[:, e].bitcast(F32),
                                        ALU.subtract).then_inc(w1_split, 1)

            def split_w2(e):
                pool.wait_ge(w2_in[e], 16)
                pool.wait_ge(w2_hi_ready, e + 1)
                nc.gpsimd.tensor_tensor(w2_lo[:, e], w2_f[:, e], w2_hi[:, e].bitcast(F32),
                                        ALU.subtract).then_inc(w2_lo_ready, 1)

            for e in range(6):
                split_w1(e)
            for i in range(NT):
                for k, (v, r) in enumerate(((var3, rstd3), (var4, rstd4))):
                    pool.wait_ge(var_ready, 2 + 2 * i + k + 1)
                    nc.gpsimd.tensor_tensor(r[:, i:i + 1], v[:, i:i + 1], neg_half[:, 0:1],
                                            ALU.pow).then_inc(rstd_ready, 1)
            split_w2(0)
            split_w1(6)
            split_w1(7)
            for e in range(E):
                for f in range(FT):
                    pool.wait_ge(gelu_ready, e * FT + f + 1)
                    if e >= 2:
                        pool.wait_ge(down_done, e - 1)
                    nc.gpsimd.tensor_scalar(hid_hi[:, e % 2, f], hid[:, e % 2, f], 1.0, 0.0,
                                            ALU.mult, ALU.add).then_inc(hi_ready, 1)
                if e + 1 < E:
                    split_w2(e + 1)

        @block.scalar
        def _(act):
            act.dma_start(ends_i[:], end_ids.to_broadcast([P, 2])).then_inc(end_in, 16)
            act.dma_start(wq_col[:], wq).then_inc(small_in, 16)
            act.dma_start(wk_col[:], wk).then_inc(small_in, 16)
            act.wait_ge(diag_zero, 1)
            for h in range(H):
                act.dma_start(wv_diag[h * HD:(h + 1) * HD, h * HD:(h + 1) * HD], wv[h]).then_inc(small_in, 16)

            def squares(i):
                if i == 0:
                    act.wait_ge(negq_ready, NT)
                for uu in range(H // 2):
                    unit = i * H // 2 + uu
                    act.wait_ge(kb_done, unit + 1)
                    for k in range(2):
                        h = 2 * uu + k
                        nc.scalar.activation(dist[:, i, :, h], ps[:, unit % KB, k * CLS:(k + 1) * CLS].rearrange("p (s c) -> p s c", s=STATES),
                                             ACT.Square, bias=neg_q[:, i, h:h + 1]).then_inc(dist_ready, 1)

            def exps(i):
                act.wait_ge(shift_ready, i + 1)
                nc.scalar.activation(prob[:, i], dist[:, i], ACT.Exp, scale=-1.0 / HD ** 0.5).then_inc(prob_ready, 1)

            def evict_pt(i):
                act.wait_ge(pt_done, 3 * i + 1)
                if i >= 2:
                    act.wait_ge(o_done, i - 1)
                nc.scalar.activation(prob_t[:, i % 2, 0], ps[:, BK_PT, :].rearrange("p (k q) -> p k q", k=PAIRS),
                                     ACT.Copy).then_inc(pt_act, 1)

            squares(0)
            squares(1)
            exps(0)
            squares(2)
            evict_pt(0)
            exps(1)
            evict_pt(1)
            exps(2)
            evict_pt(2)
            act.wait_ge(shifted_ready, 1)
            nc.scalar.activation(e_exp[:], shifted[:], ACT.Exp).then_inc(gexp_ready, 1)

            def round_w2(e):
                act.wait_ge(w2_in[e], 16)
                nc.scalar.activation(w2_hi[:, e], w2_f[:, e], ACT.Copy).then_inc(w2_hi_ready, 1)

            round_w2(0)
            act.wait_ge(small_in, 16 * SMALL)
            for e in range(E):
                if e + 1 < E:
                    round_w2(e + 1)
                for f in range(FT):
                    n = e * FT + f
                    act.wait_ge(up_done, n + 1)
                    if e >= 2:
                        act.wait_ge(hi_ready, n - 2 * FT + 1)
                        act.wait_ge(lo_ready, n - 2 * FT + 1)
                    nc.scalar.activation(hid[:, e % 2, f], ps[:, n % 4, 0:ROWS], ACT.Gelu,
                                         bias=b1_col[:, e, f:f + 1]).then_inc(gelu_ready, 1)
            for g in range(0, Y_GROUPS, 2):
                act.wait_ge(y_done, g + 1)
                nc.scalar.activation(y[:, g * 4 // J, g * 4 % J:g * 4 % J + 4],
                                     ps[:, g % 4, :].rearrange("p (j d) -> p j d", j=4), ACT.Copy).then_inc(y_act, 1)

        @block.vector
        def _(dve):
            n = 0

            def step(ins):
                nonlocal n
                n += 1
                ins.then_inc(dve_step, 1)

            def settle():
                dve.wait_ge(dve_step, n)

            V = nc.vector
            dve.wait_ge(end_in, 16)
            dve.wait_ge(consts_ready, 3)
            dve.wait_ge(pool_step, 11)
            V.tensor_copy(ident_b[:], ident[0:B * J, 0:B * J]).then_inc(ident_ready, 1)
            step(V.tensor_copy(ends_f[:], ends_i[:]))
            for b in range(B):
                for s in range(STATES):
                    step(V.tensor_copy(gather[:, b, s], ident[0:SYM, 0:SYM]))
            settle()
            for k in range(2):
                step(V.tensor_scalar(end_hot[:, k:k + 1], iota_part[0:SYM], ends_f[0:SYM, k:k + 1], 1.5,
                                     ALU.is_equal, ALU.mult))
            settle()
            for b in range(B):
                for s, k in ((1, 1), (2, 0)):
                    ins = V.tensor_scalar(gather[:, b, s], ident[0:SYM, 0:SYM], end_hot[:, k:k + 1], None, ALU.add)
                    if (b, s) == (B - 1, STATES - 1):
                        ins.then_inc(gather_ready, 1)
                    else:
                        step(ins)

            dve.wait_ge(x_in, 16)
            step(V.tensor_copy(x_f[:], x_i[:]))
            settle()
            step(V.tensor_scalar(code0[:], x_f[:], ends_f[:, 0:1], 2.0, ALU.is_equal, ALU.mult))
            settle()
            step(V.scalar_tensor_tensor(out=code[:], in0=x_f[:], scalar=ends_f[:, 1:2], in1=code0[:],
                                        op0=ALU.is_equal, op1=ALU.max))
            settle()
            step(V.tensor_scalar(no_end[:], code[:], 0.0, None, ALU.is_equal))
            settle()
            for b in range(B):
                ins = V.tensor_tensor_scan(local[:, b, ::-1], no_end[:, b, ::-1], code[:, b, ::-1], 0.0,
                                           ALU.mult, ALU.add)
                if b == B - 1:
                    ins.then_inc(total_ready, 1)
                else:
                    step(ins)

            def moments(i, src, st, m, v):
                step(V.bn_stats(st[:, i], src[:, i]))
                settle()
                step(V.bn_aggr(m[:, i], st[:, i]))
                settle()
                return V.tensor_scalar(v[:, i:i + 1], m[:, i, 1:2], EPS, None, ALU.add)

            def moments_all(src, st, m, v):
                for i in range(NT):
                    step(V.bn_stats(st[:, i], src[:, i]))
                settle()
                for i in range(NT):
                    step(V.bn_aggr(m[:, i], st[:, i]))
                settle()
                return V.tensor_scalar(v[:], m[:, :, 1], EPS, None, ALU.add)

            def normalise(i, dst, src, m, r):
                return V.tensor_scalar(dst[:, i], src[:, i], m[:, i, 0:1], r[:, i:i + 1], ALU.subtract, ALU.mult)

            dve.wait_ge(h0_done, 1)
            step(V.tensor_copy(h0[:].rearrange("p t d -> p (t d)"), ps[:, BK_H0, 0:NT * D]))
            settle()
            moments_all(h0, stats, mv, var).then_inc(var_ready, 1)
            dve.wait_ge(total_done, 1)
            step(V.tensor_copy(total_row[:], ps[0:B, BK_CNT, 0:P]))
            step(V.memset(carry_row[:, P:P + 1], 0.0))
            settle()
            step(V.tensor_scalar(total_none[:], total_row[:], 0.0, None, ALU.is_equal))
            settle()
            V.tensor_tensor_scan(carry_row[:, 0:P][:, ::-1], total_none[:, ::-1], total_row[:, ::-1], 0.0,
                                 ALU.mult, ALU.add).then_inc(carry_ready, 1)
            dve.wait_ge(rstd_ready, 1)
            for i in range(NT):
                step(normalise(i, u, h0, mv, rstd))
            settle()
            moments_all(u, stats2, mv2, var2).then_inc(var_ready, 1)

            dve.wait_ge(carry_done, 1)
            step(V.tensor_copy(carry[:], ps[:, BK_CNT, P:P + B]))
            settle()
            for b in range(B):
                step(V.tensor_tensor_scan(local[:, b, ::-1], no_end[:, b, ::-1], code[:, b, ::-1],
                                          carry[:, b:b + 1], ALU.mult, ALU.add))
            settle()
            step(V.tensor_tensor(state[:], local[:], no_end[:], ALU.mult))
            settle()
            V.scalar_tensor_tensor(out=cls[:], in0=state[:], scalar=float(SYM), in1=x_f[:], op0=ALU.mult,
                                   op1=ALU.add).then_inc(cls_ready, 1)
            dve.wait_ge(cls_ready, 1)
            step(V.tensor_scalar(state[:, 1], state[:, 1], float(STATES), None, ALU.add))
            settle()
            codes = [P, B * J, B * STATES]
            step(V.tensor_tensor(hot_code[:], state[:].rearrange("p b j -> p (b j)").unsqueeze(2).to_broadcast(codes),
                                 iota_code[:].unsqueeze(1).to_broadcast(codes), ALU.is_equal))
            syms = [P, B * J, SYM]

            dve.wait_ge(rstd_ready, 2)
            for i in range(NT):
                normalise(i, xn, u, mv2, rstd2).then_inc(xn_ready, 1)
            V.tensor_tensor(hot_sym[:], x_f[:].rearrange("p b j -> p (b j)").unsqueeze(2).to_broadcast(syms),
                            iota_sym[:].unsqueeze(1).to_broadcast(syms), ALU.is_equal).then_inc(hot_ready, 1)
            dve.wait_ge(small_in, 16 * SMALL)
            V.tensor_scalar(q_cols[:], head_mask[:], wq_col[:, 0:1], None, ALU.mult).then_inc(wqk_ready, 1)
            step(V.tensor_scalar(k_cols[:], head_mask[:], wk_col[:, 0:1], None, ALU.mult))
            settle()
            for h in range(H):
                V.tensor_scalar(k_rep[:, h], ones_rep[:], k_cols[:, h:h + 1], None, ALU.mult).then_inc(krep_ready, 1)
            dve.wait_ge(xnt_done, 1)
            V.tensor_copy(xn_t[:], ps[:, BK_XNT, 0:ROWS]).then_inc(xnt_ready, 1)
            dve.wait_ge(countrow_done, 1)
            V.tensor_copy(count_row[:], ps[0:B * STATES, BK_CNT, 192:192 + SYM]).then_inc(countrow_ready, 1)
            dve.wait_ge(countrow_ready, 1)
            step(V.tensor_scalar(is_absent[:], count_row[:], 0.0, None, ALU.is_equal))
            settle()
            dve.wait_ge(pool_step, 15)
            pens = [B * STATES, STATES, SYM]
            V.tensor_tensor(penalty[:], is_absent[:].unsqueeze(1).to_broadcast(pens),
                            state_absent[:].unsqueeze(2).to_broadcast(pens), ALU.mult).then_inc(penalty_ready, 1)
            dve.wait_ge(qv_done, 1)
            for i in range(NT):
                V.tensor_scalar(neg_q[:, i], ps[:, BK_QV, QCOL + i * H:QCOL + (i + 1) * H], -1.0, None,
                                ALU.mult).then_inc(negq_ready, 1)
            for t, a, z, first in ((0, 0, P, 0), (1, 0, HALF, P), (1, HALF, P, -HALF), (2, 0, P, HALF)):
                step(V.tensor_scalar(hot_id[a:z, t:t + 1], iota_part[a:z], float(first), None, ALU.add))
            dve.wait_ge(aug_ready, 1)
            for par in range(2):
                half = slice(par * HALF, (par + 1) * HALF)
                step(V.memset(v_aug[half, :, :, par, HD:HA], 1.0))
                for st in range(STATES):
                    step(V.tensor_copy(v_aug[half, st, :, par, 0:HD],
                                       ps[half, BK_QV, st * D:(st + 1) * D]
                                       .rearrange("p (k m e) -> p k m e", k=PAIRS, m=2)[:, :, par]))
            dve.wait_ge(count_done, 1)
            step(V.tensor_copy(count[:], ps[:, BK_CNT, 256:256 + B * STATES]))
            settle()
            for b in range(B):
                for st in range(STATES):
                    c = b * STATES + st
                    V.tensor_scalar(v_cnt[:, b, st], v_aug[:, st], count[:, c:c + 1], None, ALU.mult).then_inc(v_ready, 1)
            dve.wait_ge(clsrow_done, 1)
            V.tensor_copy(cls_row[:], ps[0:B * J, BK_CNT, 384:512]).then_inc(clsrow_ready, 1)

            def nearest(i):
                dve.wait_ge(dist_ready, H * (i + 1))
                step(V.tensor_reduce(near[:, i], dist[:, i].rearrange("p s h c -> p h s c"), AX.XY, ALU.min))
                settle()
                V.tensor_tensor(dist[:, i], dist[:, i], near[:, i].unsqueeze(1).unsqueeze(3).to_broadcast([P, STATES, H, SYM]),
                                ALU.subtract).then_inc(shift_ready, 1)

            def attend(i):
                dve.wait_ge(pt_done, 3 * i + 2)
                if i >= 2:
                    dve.wait_ge(o_done, i - 1)
                V.tensor_copy(prob_t[:, i % 2, 1], ps[:, BK_PT + 1, :].rearrange("p (k q) -> p k q", k=PAIRS)).then_inc(pt_dve, 1)
                dve.wait_ge(pt_done, 3 * i + 3)
                V.tensor_copy(prob_t[:, i % 2, 2], ps[:, BK_PT + 2, :].rearrange("p (k q) -> p k q", k=PAIRS)).then_inc(pt_dve, 1)
                dve.wait_ge(o_done, i + 1)
                o = ps[:, BK_O, 0:H * HA].rearrange("p (h e) -> p h e", h=H)
                step(V.reciprocal(rden[:, i], o[:, :, HD]))
                settle()
                V.tensor_tensor(heads[:, i], o[:, :, 0:HD], rden[:, i].unsqueeze(2).to_broadcast([P, H, HD]),
                                ALU.mult).then_inc(heads_ready, 1)
                dve.wait_ge(headst_done, i + 1)
                V.tensor_copy(heads_t[:, i], ps[:, BK_CHAIN, 0:P]).then_inc(headst_ready, 1)

            def residual(i):
                dve.wait_ge(att_done, i + 1)
                V.tensor_tensor(h1[:, i], ps[:, BK_CHAIN, P:2 * P], u[:, i], ALU.add).then_inc(att_read, 1)
                dve.wait_ge(att_read, i + 1)
                step(V.tensor_tensor(h1[:, i], h1[:, i], h0[:, i], ALU.add))
                settle()
                moments(i, h1, stats3, mv3, var3).then_inc(var_ready, 1)
                dve.wait_ge(rstd_ready, 2 + 2 * i + 1)
                step(normalise(i, w_ln, h1, mv3, rstd3))
                settle()
                moments(i, w_ln, stats4, mv4, var4).then_inc(var_ready, 1)
                step(V.tensor_tensor(acc[:, i], h1[:, i], w_ln[:, i], ALU.add))
                dve.wait_ge(rstd_ready, 2 + 2 * i + 2)
                normalise(i, hn, w_ln, mv4, rstd4).then_inc(hn_ready, 1)
                dve.wait_ge(hnt_done, i + 1)
                c = slice(i * P, (i + 1) * P)
                V.tensor_scalar(hn_t[:, c], ps[:, i, 0:P], g_col[:, 0:1], b_col[:, 0:1], ALU.mult,
                                ALU.add).then_inc(hnt_ready, 1)
                dve.wait_ge(hnt_ready, i + 1)
                step(V.tensor_copy(hn_hi[:, c], hn_t[:, c]))
                settle()
                V.tensor_tensor(hn_lo[:, c], hn_t[:, c], hn_hi[:, c].bitcast(F32), ALU.subtract).then_inc(split_ready, 1)
                dve.wait_ge(logit_done, i + 1)
                V.tensor_tensor(logit[:, i], ps[:, i, P:P + E], br_row[:], ALU.add).then_inc(logit_read, 1)

            nearest(0)
            nearest(1)
            attend(0)
            nearest(2)
            residual(0)
            attend(1)
            residual(1)
            attend(2)
            residual(2)

            dve.wait_ge(logit_read, NT)
            step(V.tensor_reduce(top[:, :, 0], logit[:], AX.X, ALU.max))
            settle()
            V.tensor_tensor(shifted[:], logit[:], top[:].to_broadcast([P, NT, E]), ALU.subtract).then_inc(shifted_ready, 1)
            for i in range(NT):
                other = logit[:, i].unsqueeze(1).to_broadcast([P, E, E])
                own = logit[:, i].unsqueeze(2).to_broadcast([P, E, E])
                step(V.tensor_tensor(above[:, i], other, own, ALU.is_gt))
                step(V.tensor_tensor(tie[:, i], other, own, ALU.is_equal))
            settle()
            for i in range(NT):
                step(V.tensor_tensor(tie[:, i], tie[:, i], before[:], ALU.mult))
            settle()
            step(V.tensor_tensor(above[:], above[:], tie[:], ALU.add))
            settle()
            step(V.tensor_reduce(rank[:], above[:], AX.X, ALU.add))
            settle()
            dve.wait_ge(gexp_ready, 1)
            step(V.scalar_tensor_tensor(out=chosen[:], in0=rank[:], scalar=2.0, in1=e_exp[:], op0=ALU.is_lt,
                                        op1=ALU.mult))
            settle()
            step(V.tensor_reduce(gsum[:, :, 0], chosen[:], AX.X, ALU.add))
            settle()
            step(V.reciprocal(grec[:], gsum[:]))
            settle()
            V.tensor_tensor(gate[:], chosen[:], grec[:].to_broadcast([P, NT, E]), ALU.mult).then_inc(gate_ready, 1)
            dve.wait_ge(gate_ready, 1)

            def low_halves(e):
                for f in range(FT):
                    k = e * FT + f
                    dve.wait_ge(hi_ready, k + 1)
                    V.tensor_tensor(hid_lo[:, e % 2, f], hid[:, e % 2, f], hid_hi[:, e % 2, f].bitcast(F32),
                                    ALU.subtract).then_inc(lo_ready, 1)

            def combine(e):
                dve.wait_ge(down_done, e + 1)
                if e == 0:
                    settle()
                else:
                    dve.wait_ge(down_read, NT * e)
                for i in range(NT):
                    V.scalar_tensor_tensor(out=acc[:, i], in0=ps[:, 4 + e % 2, i * D:(i + 1) * D],
                                           scalar=gate[:, i, e:e + 1], in1=acc[:, i], op0=ALU.mult,
                                           op1=ALU.add).then_inc(down_read, 1)

            def one_hot(g):
                t, j = g // (J // 4), g % (J // 4) * 4
                dve.wait_ge(bc_done, g + 1)
                V.tensor_scalar(hot[:, t, j:j + 4], ps[:, 6 + g % 2, :].rearrange("p (j t) -> p j t", j=4),
                                hot_id[:, t:t + 1], None, ALU.is_equal).then_inc(hot_out, 1)

            low_halves(0)
            dve.wait_ge(gatet_done, NT)
            V.tensor_copy(gate_t[:], ps[0:E, 6, 0:NT * P].rearrange("e (t p) -> e t p", t=NT)).then_inc(gatet_ready, 1)
            for e in range(1, E):
                low_halves(e)
                combine(e - 1)
                for g in range(2 * (e - 1), min(2 * e, HOT_STEPS)):
                    one_hot(g)
            combine(E - 1)
            dve.wait_ge(bias_done, 1)
            dve.wait_ge(down_read, NT * E)
            for i in range(NT):
                step(V.tensor_tensor(acc[:, i], acc[:, i], ps[:, 7, i * D:(i + 1) * D], ALU.add))
            settle()
            for i in range(NT):
                step(V.tensor_copy(tab_hi[:, i], acc[:, i]))
            settle()
            for i in range(NT):
                V.tensor_tensor(tab_lo[:, i], acc[:, i], tab_hi[:, i].bitcast(F32), ALU.subtract).then_inc(table_ready, 1)
            for g in range(1, Y_GROUPS, 2):
                dve.wait_ge(y_done, g + 1)
                V.tensor_copy(y[:, g * 4 // J, g * 4 % J:g * 4 % J + 4],
                              ps[:, g % 4, :].rearrange("p (j d) -> p j d", j=4)).then_inc(y_dve, 1)

        @block.tensor
        def _(pe):
            M = nc.tensor.matmul
            pe.wait_ge(emb_in, 16)
            pe.wait_ge(gather_ready, 1)
            pe.wait_ge(dve_step, 12)
            rows = gather[:].rearrange("k b s c -> k (b s c)")
            for i in range(NT):
                mm = M(ps[:, BK_H0, i * D:(i + 1) * D], rows[:, i * P:(i + 1) * P], emb[:], start=True, stop=True)
            mm.then_inc(h0_done, 1)
            pe.wait_ge(total_ready, 1)
            nc.tensor.transpose(ps[0:B, BK_CNT, 0:P], local[:, :, 0], ident[:]).then_inc(total_done, 1)
            pe.wait_ge(carry_ready, 1)
            nc.tensor.transpose(ps[:, BK_CNT, P:P + B], carry_row[:, 1:P + 1], ident[0:B, 0:B]).then_inc(carry_done, 1)
            for i in range(NT):
                pe.wait_ge(xn_ready, i + 1)
                mm = nc.tensor.transpose(ps[:, BK_XNT, i * P:(i + 1) * P], xn[:, i], ident[:])
            mm.then_inc(xnt_done, 1)
            pe.wait_ge(hot_ready, 1)
            for k in range(B * J):
                mm = M(ps[0:B * STATES, BK_CNT, 192:192 + SYM], hot_code[:, k], hot_sym[:, k],
                       start=(k == 0), stop=(k == B * J - 1))
            mm.then_inc(countrow_done, 1)
            pe.wait_ge(xnt_ready, 1)
            pe.wait_ge(wqk_ready, 1)
            pe.wait_ge(small_in, 16 * SMALL)
            for par in range(2):
                for st in range(STATES):
                    M(ps[par * HALF:(par + 1) * HALF, BK_QV, st * D:(st + 1) * D], xn_t[:, st * SYM:(st + 1) * SYM],
                      wv_diag[:], start=True, stop=True)
            for i in range(NT):
                mm = M(ps[:, BK_QV, QCOL + i * H:QCOL + (i + 1) * H], xn_t[:, i * P:(i + 1) * P], q_cols[:],
                       start=True, stop=True)
            mm.then_inc(qv_done, 1)

            def keys(unit):
                i, hh = unit // (H // 2), unit % (H // 2)
                if unit >= KB:
                    pe.wait_ge(dist_ready, 2 * (unit - KB + 1))
                for k in range(2):
                    dst = ps[:, unit % KB, k * CLS:(k + 1) * CLS]
                    M(dst, k_rep[:, 2 * hh + k], xn_t[:, 0:CLS], start=True, stop=False)
                    mm = M(dst, batch_sel[:, i], penalty[:].rearrange("k s c -> k (s c)"), start=False, stop=True)
                mm.then_inc(kb_done, 1)

            pe.wait_ge(krep_ready, H)
            pe.wait_ge(penalty_ready, 1)
            keys(0)
            pe.wait_ge(countrow_ready, 1)
            for k in range(2):
                mm = M(ps[k * HALF:(k + 1) * HALF, BK_CNT, 256:256 + B * STATES], count_row[:],
                       ident[0:B * STATES, 0:B * STATES], start=True, stop=True)
            mm.then_inc(count_done, 1)
            keys(1)
            keys(2)
            pe.wait_ge(v_ready, 1)
            pe.wait_ge(cls_ready, 1)
            nc.tensor.transpose(ps[0:B * J, BK_CNT, 384:512], cls[:].rearrange("p b j -> p (b j)"),
                                ident[:]).then_inc(clsrow_done, 1)

            def transposes(i):
                pe.wait_ge(prob_ready, i + 1)
                for st in range(STATES):
                    if i >= 1:
                        pe.wait_ge(*((pt_act, i), (pt_dve, 2 * i - 1), (pt_dve, 2 * i))[st])
                    for k in range(PAIRS):
                        mm = nc.tensor.transpose(ps[:, BK_PT + st, k * P:(k + 1) * P],
                                                 prob[:, i, st, 2 * k:2 * k + 2].rearrange("p h c -> p (h c)"), ident[:])
                    mm.then_inc(pt_done, 1)

            def weighted(i):
                pe.wait_ge(pt_act, i + 1)
                pe.wait_ge(pt_dve, 2 * (i + 1))
                pe.wait_ge(v_ready, B * STATES)
                pe.wait_ge(clsrow_ready, 1)
                if i >= 1:
                    pe.wait_ge(heads_ready, i)
                parts = ((0, 0, P),) if i == 0 else ((0, 0, HALF), (1, HALF, P)) if i == 1 else ((1, 0, P),)
                for b, a, z in parts:
                    for k in range(PAIRS):
                        for st in range(STATES):
                            mm = M(ps[a:z, BK_O, 2 * k * HA:2 * (k + 1) * HA], prob_t[:, i % 2, st, k, a:z],
                                   v_cnt[:, b, st, k].rearrange("p m e -> p (m e)"),
                                   start=(st == 0), stop=(st == STATES - 1))
                mm.then_inc(o_done, 1)

            def output(i):
                pe.wait_ge(heads_ready, i + 1)
                if i >= 1:
                    pe.wait_ge(att_read, i)
                nc.tensor.transpose(ps[:, BK_CHAIN, 0:P], heads[:, i].rearrange("p h d -> p (h d)"),
                                    ident[:]).then_inc(headst_done, 1)
                pe.wait_ge(headst_ready, i + 1)
                M(ps[:, BK_CHAIN, P:2 * P], heads_t[:, i], wm_sb[:], start=True, stop=True).then_inc(att_done, 1)

            def route(i):
                pe.wait_ge(hn_ready, i + 1)
                pe.wait_ge(dist_ready, NT * H)
                nc.tensor.transpose(ps[:, i, 0:P], hn[:, i], ident[:]).then_inc(hnt_done, 1)
                pe.wait_ge(hnt_ready, i + 1)
                M(ps[:, i, P:P + E], hn_t[:, i * P:(i + 1) * P], wr_t[:], start=True, stop=True).then_inc(logit_done, 1)

            for unit in range(3, 8):
                keys(unit)
            transposes(0)
            for unit in range(8, UNITS):
                keys(unit)
            weighted(0)
            output(0)
            transposes(1)
            route(0)
            weighted(1)
            output(1)
            transposes(2)
            route(1)
            weighted(2)
            output(2)
            route(2)

            def up(e):
                pe.wait_ge(w1_split, 2 * (e + 1))
                for f in range(FT):
                    k = e * FT + f
                    if k >= 4:
                        pe.wait_ge(gelu_ready, k - 3)
                    elif k < NT:
                        pe.wait_ge(logit_read, k + 1)
                    dst = ps[:, k % 4, 0:ROWS]
                    c = slice(f * P, (f + 1) * P)
                    M(dst, w1_hi[:, e, c], hn_hi[:], start=True, stop=False)
                    M(dst, w1_hi[:, e, c], hn_lo[:], start=False, stop=False)
                    M(dst, w1_lo[:, e, c], hn_hi[:], start=False, stop=True).then_inc(up_done, 1)

            def down(e):
                pe.wait_ge(w2_lo_ready, e + 1)
                pe.wait_ge(lo_ready, FT * (e + 1))
                if e >= 2:
                    pe.wait_ge(down_read, NT * (e - 1))
                for i in range(NT):
                    c = slice(i * P, (i + 1) * P)
                    dst = ps[:, 4 + e % 2, i * D:(i + 1) * D]
                    for f in range(FT):
                        M(dst, hid_hi[:, e % 2, f, c], w2_hi[:, e, f], start=(f == 0), stop=False)
                        M(dst, hid_hi[:, e % 2, f, c], w2_lo[:, e, f], start=False, stop=False)
                        mm = M(dst, hid_lo[:, e % 2, f, c], w2_hi[:, e, f], start=False, stop=(f == FT - 1))
                mm.then_inc(down_done, 1)

            def class_rows(g):
                t, j0 = g // (J // 4), g % (J // 4) * 4
                if g >= 2:
                    pe.wait_ge(hot_out, g - 1)
                else:
                    pe.wait_ge(gatet_ready, 1)
                for k in range(4):
                    j = j0 + k
                    if t == 1:
                        for half in range(2):
                            mm = M(ps[half * HALF:(half + 1) * HALF, 6 + g % 2, k * P:(k + 1) * P],
                                   ident_b[:, half * J + j:half * J + j + 1].to_broadcast([B * J, HALF]), cls_row[:], start=True, stop=True)
                    else:
                        mm = M(ps[:, 6 + g % 2, k * P:(k + 1) * P], ident_b[:, (t // 2) * J + j:(t // 2) * J + j + 1].to_broadcast([B * J, P]), cls_row[:],
                               start=True, stop=True)
                mm.then_inc(bc_done, 1)

            pe.wait_ge(split_ready, NT)
            up(0)
            pe.wait_ge(gate_ready, 1)
            for i in range(NT):
                nc.tensor.transpose(ps[0:E, 6, i * P:(i + 1) * P], gate[:, i], ident[:]).then_inc(gatet_done, 1)
            pe.wait_ge(ident_ready, 1)
            for e in range(1, E):
                up(e)
                down(e - 1)
                for g in range(2 * (e - 1), min(2 * e, HOT_STEPS)):
                    class_rows(g)
            pe.wait_ge(hot_out, HOT_STEPS)
            for i in range(NT):
                mm = M(ps[:, 7, i * D:(i + 1) * D], gate_t[:, i], b2_sb[:], start=True, stop=True)
            mm.then_inc(bias_done, 1)
            down(E - 1)

            pe.wait_ge(table_ready, NT)
            for g in range(Y_GROUPS):
                b, j0 = g * 4 // J, g * 4 % J
                if g >= 4:
                    pe.wait_ge(*((y_act, (g - 4) // 2 + 1) if g % 2 == 0 else (y_dve, (g - 4) // 2 + 1)))
                full, part = (0, slice(0, HALF)) if b == 0 else (2, slice(HALF, P))
                for k in range(4):
                    dst = ps[:, g % 4, k * D:(k + 1) * D]
                    for n, tab in enumerate((tab_hi, tab_lo)):
                        M(dst, hot[:, full, j0 + k], tab[:, full], start=(n == 0), stop=False)
                        mm = M(dst, hot[part, 1, j0 + k], tab[part, 1], start=False, stop=(n == 1))
                mm.then_inc(y_done, 1)


def kernel(**inputs):
    import concourse.bacc as bacc
    from concourse.bass_utils import run_bass_kernel_spmd

    pre = {k: np.asarray(v) for k, v in inputs.items()}
    laid = {
        "x": pre["x"],
        "weight": pre["L0_tok_weight"],
        "end_ids": pre["L0_tok_end_ids"].reshape(1, 2),
        "wq": pre["L0_attn_Wq"].reshape(P, 1),
        "wk": pre["L0_attn_Wk"].reshape(P, 1),
        "wv": pre["L0_attn_Wv"],
        "wm": pre["L0_attn_Wm"],
        "ln_g": pre["L0_ffn_ln_g"].reshape(P, 1),
        "ln_b": pre["L0_ffn_ln_b"].reshape(P, 1),
        "w_r": pre["L0_ffn_w_r"].T,
        "b_r": pre["L0_ffn_b_r"].reshape(1, E),
        "w1": pre["L0_ffn_W1"],
        "b1": pre["L0_ffn_b1"].reshape(E, FT, P).transpose(2, 0, 1),
        "w2": pre["L0_ffn_W2"],
        "b2": pre["L0_ffn_b2"],
    }
    nc = bacc.Bacc("TRN2", target_bir_lowering=False, num_devices=1)
    arrays, args = {}, []
    for name, a in laid.items():
        a = np.ascontiguousarray(a)
        arrays[f"in_{name}"] = a
        args.append(nc.dram_tensor(f"in_{name}", a.shape, mybir.dt.from_np(a.dtype), kind="ExternalInput").ap())
    args.append(nc.dram_tensor("out_y", (B, T, D), F32, kind="ExternalOutput").ap())
    build(nc, *args)
    r = run_bass_kernel_spmd(nc, [arrays], core_ids=[0])
    return r.results[0]["out_y"]
```

```python
from contextlib import ExitStack

import numpy as np

import concourse.bass as bass
from concourse import mybir

F32 = mybir.dt.float32
F32R = mybir.dt.float32r
BF16 = mybir.dt.bfloat16
I32 = mybir.dt.int32
ALU = mybir.AluOpType
ACT = mybir.ActivationFunctionType
AX = mybir.AxisListType

P = 128
B, T, D = 2, 2048, 128
SYM = 64
STATES = 3
CLS = STATES * SYM
ROWS = B * CLS
NT = ROWS // P
H, HD = 8, 16
HA = HD + 1
E, DH = 8, 512
FT = DH // P
J = T // P
EPS = 1e-5
HALF = 64
PAIRS = H // 2
ABSENT = 1e18
BANK = 512
UNITS = NT * PAIRS


def build(nc, x, weight, end_ids, wq, wk, wv, wm, ln_g, ln_b, w_r, b_r, w1, b1, w2, b2, out):
    ctx = ExitStack()
    with ctx:
        def sb(name, shape, dt=F32):
            return ctx.enter_context(nc.sbuf_tensor(name, shape, dt))

        def sem(name):
            return ctx.enter_context(nc.semaphore(name))

        ps = ctx.enter_context(nc.psum_tensor("ps", [P, 8, BANK], F32))

        x_i = sb("x_i", [P, B, J], I32)
        ends_i = sb("ends_i", [P, 2], I32)
        emb = sb("emb", [SYM, D])
        wq_col = sb("wq_col", [P, 1])
        wk_col = sb("wk_col", [P, 1])
        wv_diag = sb("wv_diag", [P, D])
        wm_sb = sb("wm_sb", [P, D])
        g_col = sb("g_col", [P, 1])
        b_col = sb("b_col", [P, 1])
        wr_t = sb("wr_t", [P, E])
        br_row = sb("br_row", [P, E])
        b1_col = sb("b1_col", [P, E, FT])
        b2_col = sb("b2_col", [P, E])
        w1_f = sb("w1_f", [P, E, DH])
        w2_f = sb("w2_f", [P, E, FT, D])
        w1_hi = sb("w1_hi", [P, E, DH], F32R)
        w1_lo = sb("w1_lo", [P, E, DH], F32R)
        w2_hi = sb("w2_hi", [P, E, FT, D], F32R)
        w2_lo = sb("w2_lo", [P, E, FT, D], F32R)

        ident = sb("ident", [P, P])
        ident_b = sb("ident_b", [B * J, B * J], BF16)
        ident_r = sb("ident_r", [B * H, B * H], F32R)
        mixed_sel = sb("mixed_sel", [B * H, H, P], F32R)
        iota_sym = sb("iota_sym", [P, SYM, B * J], BF16)
        iota_part = sb("iota_part", [P, 1])
        iota_code = sb("iota_code", [P, B * STATES])
        hot_id = sb("hot_id", [P, NT])
        head_mask = sb("head_mask", [P, H])
        batch_sel = sb("batch_sel", [B * STATES, B, H], BF16)
        state_absent = sb("state_absent", [B * STATES, STATES])
        before = sb("before", [P, E, E])
        neg_half = sb("neg_half", [P, NT])
        warm = sb("warm", [P, 1])

        x_f = sb("x_f", [P, B, J])
        x_b = sb("x_b", [P, B * J], BF16)
        ends_f = sb("ends_f", [P, 2])
        code0 = sb("code0", [P, B, J])
        code = sb("code", [P, B, J])
        no_end = sb("no_end", [P, B, J])
        local = sb("local", [P, B, J])
        final = sb("final", [P, B, J])
        state = sb("state", [P, B, J])
        cls = sb("cls", [P, B, J])
        hot_code = sb("hot_code", [P, B * J, B * STATES], BF16)
        total_row = sb("total_row", [B, P])
        total_none = sb("total_none", [B, P])
        carry_row = sb("carry_row", [B, P + 1])
        carry = sb("carry", [P, B])
        count_row = sb("count_row", [B * STATES, SYM])
        is_absent = sb("is_absent", [B * STATES, SYM])
        penalty = sb("penalty", [B * STATES, STATES, SYM], BF16)
        count = sb("count", [P, B * STATES])
        cls_row = sb("cls_row", [B * J, P], BF16)
        hot = sb("hot", [P, NT, J, P], F32R)

        end_hot = sb("end_hot", [SYM, 4])
        gather = sb("gather", [SYM, 4, SYM])
        stats = sb("stats", [P, NT, 6])
        mv = sb("mv", [P, NT, 2])
        var = sb("var", [P, 2, NT])
        rstd = sb("rstd", [P, 2, NT])
        xn = sb("xn", [P, 2, D])
        xn_t = sb("xn_t", [P, 2 * P])
        h0 = sb("h0", [P, NT, D])
        u_h0 = sb("u_h0", [P, NT, D])
        q_cols = sb("q_cols", [P, H])
        k_cols = sb("k_cols", [P, B, H])
        key_hi = sb("key_hi", [B * H, CLS], F32R)
        key_lo = sb("key_lo", [B * H, CLS], F32R)
        neg_q = sb("neg_q", [P, NT, H])
        v_aug = sb("v_aug", [P, STATES, PAIRS, 2, HA])
        v_cnt = sb("v_cnt", [P, PAIRS, STATES, B, 2, HA])
        RING = 4
        dist = sb("dist", [P, RING, STATES, 2, SYM])
        near = sb("near", [P, UNITS, 2])
        shift = sb("shift", [P, UNITS, 2])
        prob_t = sb("prob_t", [P, RING, STATES, P])
        hot_sym = (prob_t[:].rearrange("p r s q -> p (r s q)")[:, 0:SYM * B * J // 2].bitcast(BF16)
                   .rearrange("p (c t) -> p c t", c=SYM))
        rden = sb("rden", [P, NT, PAIRS, 2])
        heads = sb("heads", [P, NT, PAIRS, 2, HD])
        heads_t = sb("heads_t", [P, NT, P])
        h1 = sb("h1", [P, NT, D])
        stats3 = sb("stats3", [P, NT, 6])
        mv3 = sb("mv3", [P, NT, 2])
        var3 = sb("var3", [P, NT, 2])
        rstd3 = sb("rstd3", [P, NT, 2])
        hn = sb("hn", [P, NT, D])
        hn_t = sb("hn_t", [P, ROWS])
        hn_hi = sb("hn_hi", [P, ROWS], F32R)
        hn_lo = sb("hn_lo", [P, ROWS], F32R)

        logit = sb("logit", [P, NT, E])
        above = sb("above", [P, NT, E, E])
        tie = sb("tie", [P, NT, E, E])
        rank = sb("rank", [P, NT, E])
        top = sb("top", [P, NT, 1])
        shifted = sb("shifted", [P, NT, E])
        e_exp = sb("e_exp", [P, NT, E])
        chosen = sb("chosen", [P, NT, E])
        gsum = sb("gsum", [P, NT, 1])
        grec = sb("grec", [P, NT, 1])
        gate = sb("gate", [P, NT, E])
        gate_t = sb("gate_t", [E, ROWS])
        gate_hi = sb("gate_hi", [E, ROWS], F32R)
        gate_lo = sb("gate_lo", [E, ROWS], F32R)

        hid_hi = sb("hid_hi", [P, 2, FT, ROWS], F32R)
        hid_lo = sb("hid_lo", [P, 2, FT, ROWS], F32R)
        w1_flat = w1_f[:].rearrange("p e f -> p (e f)")
        hid = w1_flat[:, 0:2 * FT * ROWS].rearrange("p (k t r) -> p k t r", k=2, t=FT)
        base = w1_flat[:, 2 * FT * ROWS:2 * FT * ROWS + ROWS].rearrange("p (t d) -> p t d", t=NT)
        w_ln = w1_flat[:, 2 * FT * ROWS + ROWS:2 * FT * ROWS + 2 * ROWS].rearrange("p (t d) -> p t d", t=NT)
        w2_flat = w2_f[:].rearrange("p e t d -> p (e t d)")
        down_sb = w2_flat[:, 0:2 * ROWS].rearrange("p (k r) -> p k r", k=2)
        term = w2_flat[:, 2 * ROWS:4 * ROWS].rearrange("p (k r) -> p k r", k=2)
        acc = w2_flat[:, 4 * ROWS:5 * ROWS]
        table = w2_flat[:, 5 * ROWS:6 * ROWS].rearrange("p (t d) -> p t d", t=NT)
        tab = sb("tab", [P, NT, 2, D], F32R)
        y = w1_f[:].rearrange("p e (j d) -> p (e j) d", d=D).rearrange("p (b j) d -> p b j d", b=B)

        x_in = sem("x_in")
        end_in = sem("end_in")
        emb_in = sem("emb_in")
        qk_in = sem("qk_in")
        wv_in = sem("wv_in")
        small_in = sem("small_in")
        w1_in = [sem(f"w1_in{i}") for i in range(4)]
        w2_in = [sem(f"w2_in{i}") for i in range(4)]
        y_out = sem("y_out")
        pool_step = sem("pool_step")
        ident_ready = sem("ident_ready")
        mask_ready = sem("mask_ready")
        iota_ready = sem("iota_ready")
        select_ready = sem("select_ready")
        diag_zero = sem("diag_zero")
        aug_zero = sem("aug_zero")
        small_ident = sem("small_ident")
        gather_ready = sem("gather_ready")
        h0_done = sem("h0_done")
        var_ready = sem("var_ready")
        rstd_ready = sem("rstd_ready")
        var3_ready = sem("var3_ready")
        rstd3_ready = sem("rstd3_ready")
        xn_ready = sem("xn_ready")
        xnt_done = sem("xnt_done")
        xnt_ready = sem("xnt_ready")
        qk_cols = sem("qk_cols")
        qv_done = sem("qv_done")
        negq_ready = sem("negq_ready")
        total_ready = sem("total_ready")
        total_done = sem("total_done")
        carry_ready = sem("carry_ready")
        carry_done = sem("carry_done")
        hot_ready = sem("hot_ready")
        countrow_done = sem("countrow_done")
        countrow_ready = sem("countrow_ready")
        penalty_ready = sem("penalty_ready")
        keyrow_done = sem("keyrow_done")
        key_split = sem("key_split")
        count_done = sem("count_done")
        count_ready = sem("count_ready")
        cls_ready = sem("cls_ready")
        clsrow_done = sem("clsrow_done")
        clsrow_ready = sem("clsrow_ready")
        v_ready = sem("v_ready")
        kb_done = sem("kb_done")
        dist_ready = sem("dist_ready")
        near_ready = sem("near_ready")
        prob_ready = sem("prob_ready")
        pt_done = sem("pt_done")
        pt_act = sem("pt_act")
        pt_dve = sem("pt_dve")
        o_done = sem("o_done")
        heads_ready = sem("heads_ready")
        headst_done = sem("headst_done")
        headst_ready = sem("headst_ready")
        att_done = sem("att_done")
        att_read = sem("att_read")
        hn_ready = sem("hn_ready")
        hnt_done = sem("hnt_done")
        hnt_ready = sem("hnt_ready")
        hn_split = sem("hn_split")
        logit_done = sem("logit_done")
        logit_read = sem("logit_read")
        shifted_ready = sem("shifted_ready")
        gexp_ready = sem("gexp_ready")
        gate_ready = sem("gate_ready")
        gatet_done = sem("gatet_done")
        gate_split = sem("gate_split")
        w1_hi_ready = sem("w1_hi_ready")
        w1_lo_ready = sem("w1_lo_ready")
        w2_hi_ready = sem("w2_hi_ready")
        w2_lo_ready = sem("w2_lo_ready")
        up_done = sem("up_done")
        gelu_ready = sem("gelu_ready")
        hi_ready = sem("hi_ready")
        lo_ready = sem("lo_ready")
        down_done = sem("down_done")
        down_ready = sem("down_ready")
        gateb_done = sem("gateb_done")
        term_ready = sem("term_ready")
        acc_ready = sem("acc_ready")
        bc_done = sem("bc_done")
        hot_out = sem("hot_out")
        mixed_done = sem("mixed_done")
        table_ready = sem("table_ready")
        y_done = sem("y_done")
        y_hi = sem("y_hi")
        y_ready = sem("y_ready")
        dve_step = sem("dve_step")

        BK_H0, BK_XNT, BK_QV, BK_CNT, BK_CHAIN, BK_PT, BK_O = 4, 5, 6, 7, 3, 4, 7
        KB = 3
        QCOL = STATES * D
        TILE_COLS = (slice(0, P), slice(P, 2 * P), slice(HALF, HALF + P))
        PARTS = (((0, 0, P),), ((0, 0, HALF), (1, HALF, P)), ((1, 0, P),))
        HOT_STEPS = NT * J // 4
        Y_GROUPS = B * J // 2
        SMALL = 7

        def by_act(unit):
            return unit % 3 == 0

        def acts_before(unit):
            return len([k for k in range(unit) if by_act(k)])

        def pt_taken(eng, unit):
            if by_act(unit):
                eng.wait_ge(pt_act, acts_before(unit) + 1)
            else:
                eng.wait_ge(pt_dve, unit - acts_before(unit) + 1)

        block = ctx.enter_context(nc.Block())

        @block.sync
        def _(sp):
            sp.dma_start(x_i[:], x.rearrange("b (p j) -> p b j", p=P)).then_inc(x_in, 16)
            for i in range(4):
                sp.dma_start(w1_f[:, 2 * i:2 * i + 2, :],
                             w1[2 * i:2 * i + 2].rearrange("e d f -> d e f")).then_inc(w1_in[i], 16)
            for dst, src in ((wm_sb[:], wm), (g_col[:], ln_g), (b_col[:], ln_b), (wr_t[:], w_r),
                             (br_row[:], b_r.to_broadcast([P, E])), (b2_col[:], b2), (b1_col[:], b1)):
                sp.dma_start(dst, src).then_inc(small_in, 16)
            for i in range(4):
                for e in (2 * i, 2 * i + 1):
                    sp.dma_start(w2_f[:, e], w2[e].rearrange("(t f) d -> f t d", f=P)).then_inc(w2_in[i], 16)
            for g in range(0, Y_GROUPS, 2):
                b, j = g * 2 // J, g * 2 % J
                sp.wait_ge(y_ready, g + 2)
                sp.dma_start(out[b].rearrange("(p j) d -> p j d", j=J)[:, j:j + 4, :],
                             y[:, b, j:j + 4, :]).then_inc(y_out, 16)
            sp.wait_ge(y_out, 16 * Y_GROUPS // 2)

        @block.gpsimd
        def _(pool):
            n = 0

            def step(ins):
                nonlocal n
                n += 1
                ins.then_inc(pool_step, 1)

            def settle():
                pool.wait_ge(pool_step, n)

            G = nc.gpsimd
            step(G.memset(ident[:], 0.0))
            G.memset(wv_diag[:], 0.0).then_inc(diag_zero, 1)
            step(G.memset(head_mask[:], 1.0))
            settle()
            G.affine_select(out=ident[:], in_=ident[:], compare_op=ALU.not_equal, fill=1.0,
                            base=0, pattern=[[-1, P]], channel_multiplier=1).then_inc(ident_ready, 1)
            G.iota(iota_part[:], pattern=[[0, 1]], base=0, channel_multiplier=1,
                   allow_small_or_imprecise_dtypes=True).then_inc(ident_ready, 1)
            step(G.affine_select(out=head_mask[:], in_=head_mask[:], compare_op=ALU.is_ge, fill=0.0,
                                 base=0, pattern=[[-HD, H]], channel_multiplier=1))
            settle()
            G.affine_select(out=head_mask[:], in_=head_mask[:], compare_op=ALU.is_ge, fill=0.0,
                            base=HD - 1, pattern=[[HD, H]], channel_multiplier=-1).then_inc(mask_ready, 1)
            G.iota(iota_code[:], pattern=[[1, B * STATES]], base=0, channel_multiplier=0,
                   allow_small_or_imprecise_dtypes=True).then_inc(iota_ready, 1)
            G.iota(iota_sym[:], pattern=[[1, SYM], [0, B * J]], base=0, channel_multiplier=0,
                   allow_small_or_imprecise_dtypes=True).then_inc(iota_ready, 1)
            step(G.memset(neg_half[:], -0.5))
            step(G.memset(batch_sel[:], 1.0))
            step(G.memset(state_absent[:], 0.0))
            step(G.memset(before[:], 1.0))
            settle()
            step(G.affine_select(out=batch_sel[:, 0], in_=batch_sel[:, 0], compare_op=ALU.is_ge, fill=0.0,
                                 base=STATES - 1, pattern=[[0, H]], channel_multiplier=-1))
            step(G.affine_select(out=batch_sel[:, 1], in_=batch_sel[:, 1], compare_op=ALU.is_ge, fill=0.0,
                                 base=-STATES, pattern=[[0, H]], channel_multiplier=1))
            for b in range(B):
                step(G.affine_select(out=state_absent[:], in_=state_absent[:], compare_op=ALU.not_equal,
                                     fill=ABSENT, base=-STATES * b, pattern=[[-1, STATES]],
                                     channel_multiplier=1))
                settle()
            G.affine_select(out=before[:], in_=before[:], compare_op=ALU.is_gt, fill=0.0, base=0,
                            pattern=[[1, E], [-1, E]], channel_multiplier=0).then_inc(select_ready, 1)
            G.memset(v_aug[:], 0.0).then_inc(aug_zero, 1)
            pool.wait_ge(var_ready, 1)
            G.tensor_tensor(rstd[:, 1, 0:2], var[:, 1, 0:2], neg_half[:, 0:2], ALU.pow).then_inc(rstd_ready, 1)

            def low_w1(e):
                pool.wait_ge(w1_hi_ready, e + 1)
                G.tensor_tensor(w1_lo[:, e], w1_f[:, e], w1_hi[:, e].bitcast(F32), ALU.subtract).then_inc(w1_lo_ready, 1)

            def low_w2(e):
                pool.wait_ge(w2_hi_ready, e + 1)
                G.tensor_tensor(w2_lo[:, e], w2_f[:, e], w2_hi[:, e].bitcast(F32), ALU.subtract).then_inc(w2_lo_ready, 1)

            def roots(i):
                for k in (1, 0):
                    pool.wait_ge(var3_ready, 2 * i + 2 - k)
                    G.tensor_tensor(rstd3[:, i, k:k + 1], var3[:, i, k:k + 1], neg_half[:, 0:1],
                                    ALU.pow).then_inc(rstd3_ready, 1)

            low_w1(0)
            pool.wait_ge(var_ready, 2)
            G.tensor_tensor(rstd[:, 0], var[:, 0], neg_half[:], ALU.pow).then_inc(rstd_ready, 1)
            for e in range(1, E):
                low_w1(e)
            roots(0)
            low_w2(0)
            low_w2(1)
            low_w2(2)
            roots(1)
            low_w2(3)
            low_w2(4)
            roots(2)
            for e in range(5, E):
                low_w2(e)
            for e in range(E):
                for f in range(FT):
                    pool.wait_ge(gelu_ready, e * FT + f + 1)
                    if e >= 2:
                        pool.wait_ge(down_done, e - 1)
                    G.tensor_scalar(hid_hi[:, e % 2, f], hid[:, e % 2, f], 1.0, 0.0,
                                    ALU.mult, ALU.add).then_inc(hi_ready, 1)
                if e >= 3:
                    pool.wait_ge(term_ready, e - 1)
                    if e >= 4:
                        pool.wait_ge(acc_ready, e - 3)
                    G.tensor_tensor(acc, acc, term[:, e % 2], ALU.add).then_inc(acc_ready, 1)
            pool.wait_ge(term_ready, E - 1)
            pool.wait_ge(acc_ready, E - 3)
            G.tensor_tensor(acc, acc, term[:, E % 2], ALU.add).then_inc(acc_ready, 1)

        @block.scalar
        def _(act):
            act.dma_start(ends_i[:], end_ids.to_broadcast([P, 2])).then_inc(end_in, 16)
            act.dma_start(emb[:], weight).then_inc(emb_in, 16)
            act.dma_start(wk_col[:], wk).then_inc(qk_in, 16)
            act.dma_start(wq_col[:], wq).then_inc(qk_in, 16)
            act.wait_ge(diag_zero, 1)
            for h in range(H):
                act.dma_start(wv_diag[h * HD:(h + 1) * HD, h * HD:(h + 1) * HD], wv[h]).then_inc(wv_in, 16)
            act.wait_ge(ident_ready, 2)
            nc.scalar.activation(warm[:], iota_part[:], ACT.Exp, scale=-1.0)

            def high_w1(e):
                act.wait_ge(w1_in[e // 2], 16)
                nc.scalar.activation(w1_hi[:, e], w1_f[:, e], ACT.Copy).then_inc(w1_hi_ready, 1)

            def high_w2(e):
                act.wait_ge(w2_in[e // 2], 32)
                nc.scalar.activation(w2_hi[:, e], w2_f[:, e], ACT.Copy).then_inc(w2_hi_ready, 1)

            def squares(unit):
                i, k = unit // PAIRS, unit % PAIRS
                act.wait_ge(kb_done, unit + 1)
                if unit >= RING:
                    act.wait_ge(pt_done, unit - RING + 1)
                for m in range(2):
                    h = 2 * k + m
                    nc.scalar.activation(dist[:, unit % RING, :, m],
                                         ps[:, unit % KB, m * CLS:(m + 1) * CLS].rearrange("p (s c) -> p s c", s=STATES),
                                         ACT.Square, bias=neg_q[:, i, h:h + 1]).then_inc(dist_ready, 1)

            def exps(unit):
                act.wait_ge(near_ready, unit + 1)
                for m in range(2):
                    d = dist[:, unit % RING, :, m]
                    nc.scalar.activation(d, d, ACT.Exp, scale=-1.0 / HD ** 0.5,
                                         bias=shift[:, unit, m:m + 1]).then_inc(prob_ready, 1)

            def take(unit):
                if by_act(unit):
                    act.wait_ge(pt_done, unit + 1)
                    if unit >= RING:
                        act.wait_ge(o_done, unit - RING + 1)
                    nc.scalar.activation(prob_t[:, unit % RING], ps[:, BK_PT + unit % 3, 0:STATES * P]
                                         .rearrange("p (s q) -> p s q", s=STATES), ACT.Copy).then_inc(pt_act, 1)

            for e in range(E):
                high_w1(e)
            act.wait_ge(negq_ready, NT)
            squares(0)
            squares(1)
            for unit in range(UNITS):
                if unit + 2 < UNITS:
                    squares(unit + 2)
                exps(unit)
                if unit >= 1:
                    take(unit - 1)
                if unit >= 4:
                    high_w2(unit - 4)
            take(UNITS - 1)
            act.wait_ge(shifted_ready, 1)
            nc.scalar.activation(e_exp[:], shifted[:], ACT.Exp).then_inc(gexp_ready, 1)
            act.wait_ge(small_in, 16 * SMALL)

            def take_down(e):
                act.wait_ge(down_done, e + 1)
                if e >= 2:
                    act.wait_ge(term_ready, e - 1)
                nc.scalar.activation(down_sb[:, e % 2], ps[:, 4 + e % 2, 0:ROWS], ACT.Identity,
                                     bias=b2_col[:, e:e + 1]).then_inc(down_ready, 1)

            for e in range(E):
                for f in range(FT):
                    n = e * FT + f
                    act.wait_ge(up_done, n + 1)
                    if e >= 2:
                        act.wait_ge(hi_ready, n - 2 * FT + 1)
                        act.wait_ge(lo_ready, n - 2 * FT + 1)
                    nc.scalar.activation(hid[:, e % 2, f], ps[:, n % 4, 0:ROWS], ACT.Gelu,
                                         bias=b1_col[:, e, f:f + 1]).then_inc(gelu_ready, 1)
                if e >= 1:
                    take_down(e - 1)
            take_down(E - 1)
            for g in range(Y_GROUPS):
                act.wait_ge(y_done, g + 1)
                nc.scalar.activation(y[:, g * 2 // J, g * 2 % J:g * 2 % J + 2],
                                     ps[:, g % 8, :].rearrange("p (j k d) -> p j k d", j=2, k=2)[:, :, 0],
                                     ACT.Copy).then_inc(y_hi, 1)

        @block.vector
        def _(dve):
            n = 0

            def step(ins):
                nonlocal n
                n += 1
                ins.then_inc(dve_step, 1)

            def settle():
                dve.wait_ge(dve_step, n)

            V = nc.vector
            step(V.memset(end_hot[:], 0.0))
            dve.wait_ge(end_in, 16)
            step(V.tensor_copy(ends_f[:], ends_i[:]))
            dve.wait_ge(ident_ready, 2)
            settle()
            for s, k in ((1, 1), (2, 0)):
                step(V.tensor_scalar(end_hot[:, s:s + 1], iota_part[0:SYM], ends_f[0:SYM, k:k + 1], 1.5,
                                     ALU.is_equal, ALU.mult))
            settle()
            blocks = [SYM, 4, SYM]
            V.tensor_tensor(gather[:], ident[0:SYM, 0:SYM].unsqueeze(1).to_broadcast(blocks),
                            end_hot[:].unsqueeze(2).to_broadcast(blocks), ALU.add).then_inc(gather_ready, 1)

            dve.wait_ge(x_in, 16)
            step(V.tensor_copy(x_f[:], x_i[:]))
            settle()
            step(V.tensor_scalar(code0[:], x_f[:], ends_f[:, 0:1], 2.0, ALU.is_equal, ALU.mult))
            settle()
            step(V.scalar_tensor_tensor(out=code[:], in0=x_f[:], scalar=ends_f[:, 1:2], in1=code0[:],
                                        op0=ALU.is_equal, op1=ALU.max))
            settle()
            step(V.tensor_scalar(no_end[:], code[:], 0.0, None, ALU.is_equal))
            settle()
            for b in range(B):
                V.tensor_tensor_scan(local[:, b, ::-1], no_end[:, b, ::-1], code[:, b, ::-1], 0.0,
                                     ALU.mult, ALU.add).then_inc(total_ready, 1)
            step(V.tensor_copy(x_b[:], x_f[:].rearrange("p b j -> p (b j)")))
            dve.wait_ge(qk_in, 32)
            dve.wait_ge(mask_ready, 1)
            V.tensor_scalar(q_cols[:], head_mask[:], wq_col[:, 0:1], None, ALU.mult).then_inc(qk_cols, 1)
            for b in range(B):
                V.tensor_scalar(k_cols[:, b], head_mask[:], wk_col[:, 0:1], None, ALU.mult).then_inc(qk_cols, 1)

            def moments(src, i, st, m):
                step(V.bn_stats(st[:, i], src))
                settle()
                step(V.bn_aggr(m[:, i], st[:, i]))
                settle()

            dve.wait_ge(h0_done, 1)
            rows = ps[:, BK_H0, 0:NT * D].rearrange("p (t d) -> p t d", t=NT)
            for i in range(2):
                step(V.bn_stats(stats[:, i], rows[:, i]))
            settle()
            for i in range(2):
                step(V.bn_aggr(mv[:, i], stats[:, i]))
            settle()
            V.tensor_scalar(var[:, 1, 0:2], mv[:, 0:2, 1], 1.0 + EPS, EPS * EPS, ALU.mult, ALU.add).then_inc(var_ready, 1)
            dve.wait_ge(total_done, 1)
            step(V.tensor_copy(total_row[:], ps[0:B, BK_CNT, 0:P]))
            step(V.memset(carry_row[:, P:P + 1], 0.0))
            settle()
            step(V.tensor_scalar(total_none[:], total_row[:], 0.0, None, ALU.is_equal))
            settle()
            V.tensor_tensor_scan(carry_row[:, 0:P][:, ::-1], total_none[:, ::-1], total_row[:, ::-1], 0.0,
                                 ALU.mult, ALU.add).then_inc(carry_ready, 1)
            step(V.tensor_copy(h0[:], rows))
            settle()
            dve.wait_ge(rstd_ready, 1)
            for i in range(2):
                V.tensor_scalar(xn[:, i], h0[:, i], mv[:, i, 0:1], rstd[:, 1, i:i + 1], ALU.subtract,
                                ALU.mult).then_inc(xn_ready, 1)
            dve.wait_ge(carry_done, 1)
            step(V.tensor_copy(carry[:], ps[:, BK_CNT, P:P + B]))
            settle()
            for b in range(B):
                step(V.tensor_tensor_scan(final[:, b, ::-1], no_end[:, b, ::-1], code[:, b, ::-1],
                                          carry[:, b:b + 1], ALU.mult, ALU.add))
            settle()
            step(V.tensor_tensor(state[:], final[:], no_end[:], ALU.mult))
            settle()
            V.scalar_tensor_tensor(out=cls[:], in0=state[:], scalar=float(SYM), in1=x_f[:], op0=ALU.mult,
                                   op1=ALU.add).then_inc(cls_ready, 1)
            dve.wait_ge(cls_ready, 1)
            step(V.tensor_scalar(state[:, 1], state[:, 1], float(STATES), None, ALU.add))
            settle()
            dve.wait_ge(iota_ready, 2)
            codes = [P, B * J, B * STATES]
            V.tensor_tensor(hot_code[:], state[:].rearrange("p b j -> p (b j)").unsqueeze(2).to_broadcast(codes),
                            iota_code[:].unsqueeze(1).to_broadcast(codes), ALU.is_equal).then_inc(hot_ready, 1)
            dve.wait_ge(xnt_done, 1)
            V.tensor_copy(xn_t[:], ps[:, BK_XNT, 0:2 * P]).then_inc(xnt_ready, 1)
            V.tensor_tensor(hot_sym, x_b[:].unsqueeze(1).to_broadcast([P, SYM, B * J]), iota_sym[:],
                            ALU.is_equal).then_inc(hot_ready, 1)
            V.tensor_copy(ident_b[:], ident[0:B * J, 0:B * J]).then_inc(small_ident, 1)
            V.tensor_copy(ident_r[:], ident[0:B * H, 0:B * H]).then_inc(small_ident, 1)
            dve.wait_ge(qv_done, 1)
            for i in range(NT):
                V.tensor_scalar(neg_q[:, i], ps[:, BK_QV, QCOL + i * H:QCOL + (i + 1) * H], -1.0, None,
                                ALU.mult).then_inc(negq_ready, 1)
            dve.wait_ge(select_ready, 1)
            dve.wait_ge(countrow_done, 1)
            V.tensor_copy(count_row[:], ps[0:B * STATES, BK_CNT, 192:192 + SYM]).then_inc(countrow_ready, 1)
            dve.wait_ge(countrow_ready, 1)
            step(V.tensor_scalar(is_absent[:], count_row[:], 0.0, None, ALU.is_equal))
            settle()
            pens = [B * STATES, STATES, SYM]
            V.tensor_tensor(penalty[:], is_absent[:].unsqueeze(1).to_broadcast(pens),
                            state_absent[:].unsqueeze(2).to_broadcast(pens), ALU.mult).then_inc(penalty_ready, 1)
            V.tensor_copy(mixed_sel[:].rearrange("k h (b p) -> k b h p", b=B),
                          ident[0:B * H, 0:B * H].rearrange("k (b h) -> k b h", b=B).unsqueeze(3)
                          .to_broadcast([B * H, B, H, HALF])).then_inc(small_ident, 1)
            dve.wait_ge(keyrow_done, 1)
            V.tensor_copy(key_hi[:], ps[0:B * H, BK_CHAIN, 0:CLS]).then_inc(key_split, 1)
            dve.wait_ge(key_split, 1)
            V.tensor_tensor(key_lo[:], ps[0:B * H, BK_CHAIN, 0:CLS], key_hi[:].bitcast(F32),
                            ALU.subtract).then_inc(key_split, 1)
            dve.wait_ge(aug_zero, 1)
            for par in range(2):
                half = slice(par * HALF, (par + 1) * HALF)
                step(V.memset(v_aug[half, :, :, par, HD:HA], 1.0))
                for st in range(STATES):
                    step(V.tensor_copy(v_aug[half, st, :, par, 0:HD],
                                       ps[half, BK_QV, st * D:(st + 1) * D]
                                       .rearrange("p (k m e) -> p k m e", k=PAIRS, m=2)[:, :, par]))

            def weigh_values():
                dve.wait_ge(count_done, 1)
                V.tensor_copy(count[:], ps[:, BK_CNT, 256:256 + B * STATES]).then_inc(count_ready, 1)
                dve.wait_ge(count_ready, 1)
                settle()
                for b in range(B):
                    for st in range(STATES):
                        c = b * STATES + st
                        V.tensor_scalar(v_cnt[:, :, st, b], v_aug[:, st], count[:, c:c + 1], None,
                                        ALU.mult).then_inc(v_ready, 1)
                dve.wait_ge(clsrow_done, 1)
                V.tensor_copy(cls_row[:], ps[0:B * J, BK_CNT, 384:512]).then_inc(clsrow_ready, 1)

            def rest_of_rows():
                step(V.bn_stats(stats[:, 2], h0[:, 2]))
                settle()
                step(V.bn_aggr(mv[:, 2], stats[:, 2]))
                settle()
                V.tensor_scalar(var[:, 0], mv[:, :, 1], EPS, None, ALU.add).then_inc(var_ready, 1)
                for t, a, z, first in ((0, 0, P, 0), (1, 0, HALF, P), (1, HALF, P, -HALF), (2, 0, P, HALF)):
                    step(V.tensor_scalar(hot_id[a:z, t:t + 1], iota_part[a:z], float(first), None, ALU.add))

            def residual_base(i):
                if i == 0:
                    dve.wait_ge(rstd_ready, 2)
                step(V.tensor_scalar(u_h0[:, i], h0[:, i], mv[:, i, 0:1], rstd[:, 0, i:i + 1], ALU.subtract, ALU.mult))
                settle()
                step(V.tensor_tensor(u_h0[:, i], u_h0[:, i], h0[:, i], ALU.add))

            def nearest(unit):
                dve.wait_ge(dist_ready, 2 * (unit + 1))
                step(V.tensor_reduce(near[:, unit], dist[:, unit % RING].rearrange("p s m c -> p m s c"), AX.XY, ALU.min))
                settle()
                V.tensor_scalar(shift[:, unit], near[:, unit], 1.0 / HD ** 0.5, None, ALU.mult).then_inc(near_ready, 1)

            def take(unit):
                if not by_act(unit):
                    dve.wait_ge(pt_done, unit + 1)
                    if unit >= RING:
                        dve.wait_ge(o_done, unit - RING + 1)
                    V.tensor_copy(prob_t[:, unit % RING], ps[:, BK_PT + unit % 3, 0:STATES * P]
                                  .rearrange("p (s q) -> p s q", s=STATES)).then_inc(pt_dve, 1)

            def normalise_heads(i):
                dve.wait_ge(o_done, PAIRS * (i + 1))
                for b, a, z in PARTS[i]:
                    o = ps[a:z, BK_O, 0:PAIRS * B * 2 * HA].rearrange("p (k b m e) -> p k b m e", k=PAIRS, b=B, m=2)[:, :, b]
                    step(V.reciprocal(rden[a:z, i], o[:, :, :, HD]))
                settle()
                for b, a, z in PARTS[i]:
                    o = ps[a:z, BK_O, 0:PAIRS * B * 2 * HA].rearrange("p (k b m e) -> p k b m e", k=PAIRS, b=B, m=2)[:, :, b]
                    V.tensor_tensor(heads[a:z, i], o[:, :, :, 0:HD],
                                    rden[a:z, i].unsqueeze(3).to_broadcast([z - a, PAIRS, 2, HD]),
                                    ALU.mult).then_inc(heads_ready, 3 - len(PARTS[i]))

            def turn_heads(i):
                dve.wait_ge(headst_done, i + 1)
                V.tensor_copy(heads_t[:, i], ps[:, BK_CHAIN, 0:P]).then_inc(headst_ready, 1)

            def residual(i):
                dve.wait_ge(att_done, i + 1)
                V.tensor_tensor(h1[:, i], ps[:, BK_CHAIN, P:2 * P], u_h0[:, i], ALU.add).then_inc(att_read, 1)
                dve.wait_ge(att_read, i + 1)
                moments(h1[:, i], i, stats3, mv3)
                V.tensor_scalar(var3[:, i, 1:2], mv3[:, i, 1:2], 1.0 + EPS, EPS * EPS, ALU.mult, ALU.add).then_inc(var3_ready, 1)
                V.tensor_scalar(var3[:, i, 0:1], mv3[:, i, 1:2], EPS, None, ALU.add).then_inc(var3_ready, 1)

            def double_norm(i):
                dve.wait_ge(rstd3_ready, 2 * i + 1)
                V.tensor_scalar(hn[:, i], h1[:, i], mv3[:, i, 0:1], rstd3[:, i, 1:2], ALU.subtract, ALU.mult).then_inc(hn_ready, 1)

            def split_rows(i):
                c = slice(i * P, (i + 1) * P)
                dve.wait_ge(hnt_done, i + 1)
                V.tensor_scalar(hn_t[:, c], ps[:, i, 0:P], g_col[:, 0:1], b_col[:, 0:1], ALU.mult,
                                ALU.add).then_inc(hnt_ready, 1)
                dve.wait_ge(hnt_ready, i + 1)
                V.tensor_copy(hn_hi[:, c], hn_t[:, c]).then_inc(hn_split, 1)
                dve.wait_ge(hn_split, 2 * i + 1)
                V.tensor_tensor(hn_lo[:, c], hn_t[:, c], hn_hi[:, c].bitcast(F32), ALU.subtract).then_inc(hn_split, 1)

            def read_logits(i):
                dve.wait_ge(logit_done, i + 1)
                V.tensor_tensor(logit[:, i], ps[:, i, P:P + E], br_row[:], ALU.add).then_inc(logit_read, 1)

            def base_rows(i):
                dve.wait_ge(rstd3_ready, 2 * i + 2)
                step(V.tensor_scalar(w_ln[:, i], h1[:, i], mv3[:, i, 0:1], rstd3[:, i, 0:1], ALU.subtract, ALU.mult))
                settle()
                step(V.tensor_tensor(base[:, i], h1[:, i], w_ln[:, i], ALU.add))

            after = {0: [weigh_values], 1: [rest_of_rows], 2: [lambda: residual_base(0)],
                     3: [lambda: residual_base(1)], 4: [lambda: residual_base(2)]}
            for i in range(NT - 1):
                u0 = PAIRS * (i + 1)
                after.setdefault(u0 + 1, []).append(lambda i=i: normalise_heads(i))
                after.setdefault(u0 + 2, []).append(lambda i=i: (turn_heads(i), residual(i)))
                after.setdefault(u0 + 3, []).append(lambda i=i: double_norm(i))
            dve.wait_ge(small_in, 16 * SMALL)
            for unit in range(UNITS):
                nearest(unit)
                if unit >= 2:
                    take(unit - 2)
                for what in after.get(unit, []):
                    what()
            take(UNITS - 2)
            take(UNITS - 1)
            split_rows(0)
            read_logits(0)
            split_rows(1)
            read_logits(1)
            normalise_heads(2)
            base_rows(0)
            turn_heads(2)
            residual(2)
            base_rows(1)
            double_norm(2)
            split_rows(2)
            read_logits(2)

            dve.wait_ge(logit_read, NT)
            step(V.tensor_reduce(top[:, :, 0], logit[:], AX.X, ALU.max))
            settle()
            V.tensor_tensor(shifted[:], logit[:], top[:].to_broadcast([P, NT, E]), ALU.subtract).then_inc(shifted_ready, 1)
            pairs = [P, NT, E, E]
            other = logit[:].unsqueeze(2).to_broadcast(pairs)
            own = logit[:].unsqueeze(3).to_broadcast(pairs)
            step(V.tensor_tensor(tie[:], other, own, ALU.is_equal))
            step(V.tensor_tensor(above[:], other, own, ALU.is_gt))
            settle()
            step(V.tensor_tensor(tie[:], tie[:], before[:].unsqueeze(1).to_broadcast(pairs), ALU.mult))
            settle()
            step(V.tensor_tensor(above[:], above[:], tie[:], ALU.add))
            settle()
            step(V.tensor_reduce(rank[:], above[:], AX.X, ALU.add))
            settle()
            dve.wait_ge(gexp_ready, 1)
            step(V.scalar_tensor_tensor(out=chosen[:], in0=rank[:], scalar=2.0, in1=e_exp[:], op0=ALU.is_lt,
                                        op1=ALU.mult))
            settle()
            step(V.tensor_reduce(gsum[:, :, 0], chosen[:], AX.X, ALU.add))
            settle()
            step(V.reciprocal(grec[:], gsum[:]))
            settle()
            V.tensor_tensor(gate[:], chosen[:], grec[:].to_broadcast([P, NT, E]), ALU.mult).then_inc(gate_ready, 1)

            def low_halves(e):
                for f in range(FT):
                    k = e * FT + f
                    dve.wait_ge(hi_ready, k + 1)
                    if e >= 2:
                        dve.wait_ge(down_done, e - 1)
                    V.tensor_tensor(hid_lo[:, e % 2, f], hid[:, e % 2, f], hid_hi[:, e % 2, f].bitcast(F32),
                                    ALU.subtract).then_inc(lo_ready, 1)

            def weigh(e):
                dve.wait_ge(down_ready, e + 1)
                dve.wait_ge(gateb_done, e + 1)
                if e >= 3:
                    dve.wait_ge(acc_ready, e - 2)
                V.tensor_tensor(acc if e == 0 else term[:, e % 2], ps[:, 6, 0:ROWS], down_sb[:, e % 2],
                                ALU.mult).then_inc(term_ready, 1)

            def one_hot(g):
                t, j = g // (J // 4), g % (J // 4) * 4
                dve.wait_ge(bc_done, g + 1)
                V.tensor_scalar(hot[:, t, j:j + 4], ps[:, 7, :].rearrange("p (j t) -> p j t", j=4),
                                hot_id[:, t:t + 1], None, ALU.is_equal).then_inc(hot_out, 1)

            low_halves(0)
            dve.wait_ge(gatet_done, NT)
            step(V.tensor_copy(gate_t[:], ps[0:E, 6, 0:ROWS]))
            settle()
            V.tensor_copy(gate_hi[:], gate_t[:]).then_inc(gate_split, 1)
            dve.wait_ge(gate_split, 1)
            V.tensor_tensor(gate_lo[:], gate_t[:], gate_hi[:].bitcast(F32), ALU.subtract).then_inc(gate_split, 1)
            base_rows(2)
            for e in range(1, E):
                low_halves(e)
                weigh(e - 1)
                for g in range(2 * (e - 1), min(2 * e, HOT_STEPS)):
                    one_hot(g)
            weigh(E - 1)
            for i in range(NT):
                dve.wait_ge(mixed_done, 1)
                V.tensor_tensor(table[:, i], ps[:, 7, i * D:(i + 1) * D], base[:, i], ALU.add).then_inc(table_ready, 1)
                dve.wait_ge(table_ready, 3 * i + 1)
                V.tensor_copy(tab[:, i, 0], table[:, i]).then_inc(table_ready, 1)
                dve.wait_ge(table_ready, 3 * i + 2)
                V.tensor_tensor(tab[:, i, 1], table[:, i], tab[:, i, 0].bitcast(F32), ALU.subtract).then_inc(table_ready, 1)
            for g in range(Y_GROUPS):
                dve.wait_ge(y_hi, g + 1)
                dst = y[:, g * 2 // J, g * 2 % J:g * 2 % J + 2]
                V.tensor_tensor(dst, ps[:, g % 8, :].rearrange("p (j k d) -> p j k d", j=2, k=2)[:, :, 1], dst,
                                ALU.add).then_inc(y_ready, 1)

        @block.tensor
        def _(pe):
            M = nc.tensor.matmul
            pe.wait_ge(emb_in, 16)
            pe.wait_ge(gather_ready, 1)
            cols = gather[:].rearrange("k s c -> k (s c)")
            for i in range(NT):
                mm = M(ps[:, BK_H0, i * D:(i + 1) * D], cols[:, TILE_COLS[i]], emb[:], start=True, stop=True)
            mm.then_inc(h0_done, 1)
            pe.wait_ge(total_ready, B)
            pe.wait_ge(ident_ready, 2)
            nc.tensor.transpose(ps[0:B, BK_CNT, 0:P], local[:, :, 0], ident[:]).then_inc(total_done, 1)
            pe.wait_ge(carry_ready, 1)
            nc.tensor.transpose(ps[:, BK_CNT, P:P + B], carry_row[:, 1:P + 1], ident[0:B, 0:B]).then_inc(carry_done, 1)
            for i in range(2):
                pe.wait_ge(xn_ready, i + 1)
                mm = nc.tensor.transpose(ps[:, BK_XNT, i * P:(i + 1) * P], xn[:, i], ident[:])
            mm.then_inc(xnt_done, 1)
            pe.wait_ge(xnt_ready, 1)
            pe.wait_ge(qk_cols, 1 + B)
            pe.wait_ge(wv_in, 16 * H)
            for i in range(NT):
                M(ps[:, BK_QV, QCOL + i * H:QCOL + (i + 1) * H], xn_t[:, TILE_COLS[i]], q_cols[:], start=True, stop=True)
            for par in range(2):
                for st in range(STATES):
                    mm = M(ps[par * HALF:(par + 1) * HALF, BK_QV, st * D:(st + 1) * D],
                           xn_t[:, st * SYM:(st + 1) * SYM], wv_diag[:], start=True, stop=True)
            mm.then_inc(qv_done, 1)
            pe.wait_ge(hot_ready, 2)
            for k in range(B * J):
                mm = M(ps[0:B * STATES, BK_CNT, 192:192 + SYM], hot_code[:, k], hot_sym[:, :, k],
                       start=(k == 0), stop=(k == B * J - 1))
            mm.then_inc(countrow_done, 1)
            M(ps[0:B * H, BK_CHAIN, 0:CLS], k_cols[:].rearrange("p b h -> p (b h)"), xn_t[:, 0:CLS], start=True, stop=False)
            pe.wait_ge(penalty_ready, 1)
            M(ps[0:B * H, BK_CHAIN, 0:CLS], batch_sel[:].rearrange("k b h -> k (b h)"),
              penalty[:].rearrange("k s c -> k (s c)"), start=False, stop=True).then_inc(keyrow_done, 1)

            def keys(unit):
                i, k = unit // PAIRS, unit % PAIRS
                if unit >= KB:
                    pe.wait_ge(dist_ready, 2 * (unit - KB + 1))
                for m in range(2):
                    h = 2 * k + m
                    row = i // 2 * H + h
                    sel = mixed_sel[:, h] if i == 1 else ident_r[:, row:row + 1].to_broadcast([B * H, P])
                    dst = ps[:, unit % KB, m * CLS:(m + 1) * CLS]
                    M(dst, sel, key_hi[:], start=True, stop=False)
                    mm = M(dst, sel, key_lo[:], start=False, stop=True)
                mm.then_inc(kb_done, 1)

            def turn_probs(unit):
                pe.wait_ge(prob_ready, 2 * (unit + 1))
                if unit == 2:
                    pe.wait_ge(v_ready, 1)
                if unit >= 3:
                    pt_taken(pe, unit - 3)
                for st in range(STATES):
                    mm = nc.tensor.transpose(ps[:, BK_PT + unit % 3, st * P:(st + 1) * P],
                                             dist[:, unit % RING, st].rearrange("p m c -> p (m c)"), ident[:])
                mm.then_inc(pt_done, 1)

            def weighted(unit):
                i, k = unit // PAIRS, unit % PAIRS
                pt_taken(pe, unit)
                if unit == 0:
                    pe.wait_ge(v_ready, B * STATES)
                    pe.wait_ge(clsrow_ready, 1)
                if k == 0 and i >= 1:
                    pe.wait_ge(heads_ready, 2 * i)
                b0, nb = (0, 1) if i == 0 else (0, 2) if i == 1 else (1, 1)
                c = (k * B + b0) * 2 * HA
                for st in range(STATES):
                    mm = M(ps[:, BK_O, c:c + nb * 2 * HA], prob_t[:, unit % RING, st],
                           v_cnt[:, k, st, b0:b0 + nb].rearrange("p b m e -> p (b m e)"),
                           start=(st == 0), stop=(st == STATES - 1))
                mm.then_inc(o_done, 1)

            def turn_back(i):
                pe.wait_ge(heads_ready, 2 * (i + 1))
                if i == 0:
                    pe.wait_ge(key_split, 2)
                else:
                    pe.wait_ge(att_read, i)
                nc.tensor.transpose(ps[:, BK_CHAIN, 0:P], heads[:, i].rearrange("p k m d -> p (k m d)"),
                                    ident[:]).then_inc(headst_done, 1)

            def output(i):
                pe.wait_ge(headst_ready, i + 1)
                M(ps[:, BK_CHAIN, P:2 * P], heads_t[:, i], wm_sb[:], start=True, stop=True).then_inc(att_done, 1)

            def turn_rows(i):
                pe.wait_ge(hn_ready, i + 1)
                pe.wait_ge(dist_ready, 2 * UNITS)
                nc.tensor.transpose(ps[:, i, 0:P], hn[:, i], ident[:]).then_inc(hnt_done, 1)

            def route(i):
                pe.wait_ge(hnt_ready, i + 1)
                M(ps[:, i, P:P + E], hn_t[:, i * P:(i + 1) * P], wr_t[:], start=True, stop=True).then_inc(logit_done, 1)

            pe.wait_ge(key_split, 2)
            pe.wait_ge(small_ident, 3)
            pe.wait_ge(small_in, 16 * SMALL)
            keys(0)
            keys(1)
            pe.wait_ge(countrow_ready, 1)
            for k in range(2):
                mm = M(ps[k * HALF:(k + 1) * HALF, BK_CNT, 256:256 + B * STATES], count_row[:],
                       ident[0:B * STATES, 0:B * STATES], start=True, stop=True)
            mm.then_inc(count_done, 1)
            keys(2)
            pe.wait_ge(count_ready, 1)
            nc.tensor.transpose(ps[0:B * J, BK_CNT, 384:512], cls[:].rearrange("p b j -> p (b j)"),
                                ident[:]).then_inc(clsrow_done, 1)
            chain = {}
            for i in range(NT - 1):
                u0 = PAIRS * (i + 1)
                chain[u0 + 1] = lambda i=i: turn_back(i)
                chain[u0 + 2] = lambda i=i: output(i)
            for unit in range(UNITS):
                if unit + 3 < UNITS:
                    keys(unit + 3)
                turn_probs(unit)
                if unit in chain:
                    chain[unit]()
                if unit >= 1:
                    weighted(unit - 1)
            weighted(UNITS - 1)
            turn_rows(0)
            route(0)
            turn_rows(1)
            route(1)
            turn_back(2)
            output(2)
            turn_rows(2)
            route(2)

            def up(e):
                pe.wait_ge(w1_lo_ready, e + 1)
                for f in range(FT):
                    k = e * FT + f
                    if k >= 4:
                        pe.wait_ge(gelu_ready, k - 3)
                    elif k < NT:
                        pe.wait_ge(logit_read, k + 1)
                    dst = ps[:, k % 4, 0:ROWS]
                    c = slice(f * P, (f + 1) * P)
                    M(dst, w1_hi[:, e, c], hn_hi[:], start=True, stop=False)
                    M(dst, w1_hi[:, e, c], hn_lo[:], start=False, stop=False)
                    M(dst, w1_lo[:, e, c], hn_hi[:], start=False, stop=True).then_inc(up_done, 1)

            def down(e):
                pe.wait_ge(w2_lo_ready, e + 1)
                if e >= 2:
                    pe.wait_ge(down_ready, e - 1)
                dst = ps[:, 4 + e % 2, 0:ROWS]
                for f in range(FT):
                    pe.wait_ge(lo_ready, FT * e + f + 1)
                    M(dst, w2_hi[:, e, f], hid_hi[:, e % 2, f], start=(f == 0), stop=False)
                    M(dst, w2_hi[:, e, f], hid_lo[:, e % 2, f], start=False, stop=False)
                    mm = M(dst, w2_lo[:, e, f], hid_hi[:, e % 2, f], start=False, stop=(f == FT - 1))
                mm.then_inc(down_done, 1)

            def gates(e):
                if e >= 1:
                    pe.wait_ge(term_ready, e)
                sel = ident_r[0:E, e:e + 1].to_broadcast([E, P])
                M(ps[:, 6, 0:ROWS], sel, gate_hi[:], start=True, stop=False)
                M(ps[:, 6, 0:ROWS], sel, gate_lo[:], start=False, stop=True).then_inc(gateb_done, 1)

            def class_rows(g):
                t, j0 = g // (J // 4), g % (J // 4) * 4
                if g >= 1:
                    pe.wait_ge(hot_out, g)
                for k in range(4):
                    j = j0 + k
                    if t == 1:
                        for half in range(2):
                            mm = M(ps[half * HALF:(half + 1) * HALF, 7, k * P:(k + 1) * P],
                                   ident_b[:, half * J + j:half * J + j + 1].to_broadcast([B * J, HALF]),
                                   cls_row[:], start=True, stop=True)
                    else:
                        mm = M(ps[:, 7, k * P:(k + 1) * P],
                               ident_b[:, t // 2 * J + j:t // 2 * J + j + 1].to_broadcast([B * J, P]), cls_row[:],
                               start=True, stop=True)
                mm.then_inc(bc_done, 1)

            pe.wait_ge(hn_split, 2 * NT)
            up(0)
            pe.wait_ge(gate_ready, 1)
            for i in range(NT):
                nc.tensor.transpose(ps[0:E, 6, i * P:(i + 1) * P], gate[:, i], ident[:]).then_inc(gatet_done, 1)
            for e in range(1, E):
                up(e)
                if e == 1:
                    pe.wait_ge(gate_split, 2)
                gates(e - 1)
                down(e - 1)
                for g in range(2 * (e - 1), min(2 * e, HOT_STEPS)):
                    class_rows(g)
            gates(E - 1)
            down(E - 1)
            pe.wait_ge(hot_out, HOT_STEPS)
            pe.wait_ge(acc_ready, E - 2)
            pe.wait_ge(term_ready, E)
            for i in range(NT):
                c = slice(i * P, (i + 1) * P)
                dst = ps[:, 7, i * D:(i + 1) * D]
                M(dst, acc[:, c], ident[:], start=True, stop=False)
                mm = M(dst, term[:, (E - 1) % 2, c], ident[:], start=False, stop=True)
            mm.then_inc(mixed_done, 1)

            for g in range(Y_GROUPS):
                b, j0 = g * 2 // J, g * 2 % J
                if g == 0:
                    pe.wait_ge(table_ready, 6)
                elif b == 1:
                    pe.wait_ge(table_ready, 9)
                if g == 7:
                    pe.wait_ge(table_ready, 9)
                if g >= 8:
                    pe.wait_ge(y_ready, g - 7)
                full, part = (0, slice(0, HALF)) if b == 0 else (2, slice(HALF, P))
                for k in range(2):
                    dst = ps[:, g % 8, k * 2 * D:(k + 1) * 2 * D]
                    M(dst, hot[:, full, j0 + k], tab[:, full].rearrange("p k d -> p (k d)"), start=True, stop=False)
                    mm = M(dst, hot[part, 1, j0 + k], tab[part, 1].rearrange("p k d -> p (k d)"), start=False, stop=True)
                mm.then_inc(y_done, 1)


def kernel(**inputs):
    import concourse.bacc as bacc
    from concourse.bass_utils import run_bass_kernel_spmd

    pre = {k: np.asarray(v) for k, v in inputs.items()}
    laid = {
        "x": pre["x"],
        "weight": pre["L0_tok_weight"],
        "end_ids": pre["L0_tok_end_ids"].reshape(1, 2),
        "wq": pre["L0_attn_Wq"].reshape(P, 1),
        "wk": pre["L0_attn_Wk"].reshape(P, 1),
        "wv": pre["L0_attn_Wv"],
        "wm": pre["L0_attn_Wm"],
        "ln_g": pre["L0_ffn_ln_g"].reshape(P, 1),
        "ln_b": pre["L0_ffn_ln_b"].reshape(P, 1),
        "w_r": pre["L0_ffn_w_r"].T,
        "b_r": pre["L0_ffn_b_r"].reshape(1, E),
        "w1": pre["L0_ffn_W1"],
        "b1": pre["L0_ffn_b1"].reshape(E, FT, P).transpose(2, 0, 1),
        "w2": pre["L0_ffn_W2"],
        "b2": pre["L0_ffn_b2"].T,
    }
    nc = bacc.Bacc("TRN2", target_bir_lowering=False, num_devices=1)
    arrays, args = {}, []
    for name, a in laid.items():
        a = np.ascontiguousarray(a)
        arrays[f"in_{name}"] = a
        args.append(nc.dram_tensor(f"in_{name}", a.shape, mybir.dt.from_np(a.dtype), kind="ExternalInput").ap())
    args.append(nc.dram_tensor("out_y", (B, T, D), F32, kind="ExternalOutput").ap())
    build(nc, *args)
    r = run_bass_kernel_spmd(nc, [arrays], core_ids=[0])
    return r.results[0]["out_y"]
```

```python
from contextlib import ExitStack

import numpy as np

import concourse.bass as bass
from concourse import mybir

F32 = mybir.dt.float32
F32R = mybir.dt.float32r
BF16 = mybir.dt.bfloat16
I32 = mybir.dt.int32
ALU = mybir.AluOpType
ACT = mybir.ActivationFunctionType
AX = mybir.AxisListType

P = 128
B, T, D = 2, 2048, 128
SYM = 64
STATES = 3
CLS = STATES * SYM
ROWS = B * CLS
NT = ROWS // P
H, HD = 8, 16
HA = HD + 1
LOW = 32
KR = LOW + B * H
E, DH = 8, 512
FT = DH // P
J = T // P
EPS = 1e-5
HALF = 64
PAIRS = H // 2
ABSENT = 1e18
BANK = 512
UNITS = NT * PAIRS
GR = LOW + E


def build(nc, x, weight, end_ids, columns, wv, wm, b_r, w1, ffn_columns, w2, out):
    ctx = ExitStack()
    with ctx:
        def sb(name, shape, dt=F32):
            return ctx.enter_context(nc.sbuf_tensor(name, shape, dt))

        def sem(name):
            return ctx.enter_context(nc.semaphore(name))

        ps = ctx.enter_context(nc.psum_tensor("ps", [P, 8, BANK], F32))

        x_i = sb("x_i", [P, B, J], I32)
        ends_i = sb("ends_i", [P, 2], I32)
        emb = sb("emb", [SYM, D])
        cols = sb("cols", [P, 4])
        wq_col, wk_col, g_col, b_col = (cols[:, c:c + 1] for c in range(4))
        wv_rows = sb("wv_rows", [P, HD])
        wv_diag = sb("wv_diag", [P, D])
        wm_sb = sb("wm_sb", [P, D])
        br_row = sb("br_row", [P, E])
        ffn_cols = sb("ffn_cols", [P, 2 * E + E * FT])
        wr_t, b2_col = ffn_cols[:, 0:E], ffn_cols[:, E:2 * E]
        b1_col = ffn_cols[:, 2 * E:].rearrange("p (e t) -> p e t", e=E)
        w1_f = sb("w1_f", [P, E, DH])
        w2_f = sb("w2_f", [P, E, FT, D])
        w1_hi = sb("w1_hi", [P, E, DH], F32R)
        w1_lo = sb("w1_lo", [P, E, DH], F32R)
        w2_hi = sb("w2_hi", [P, E, FT, D], F32R)
        w2_lo = sb("w2_lo", [P, E, FT, D], F32R)

        ident = sb("ident", [P, P])
        ident_b = sb("ident_b", [B * J, B * J], BF16)
        pick = sb("pick", [KR, B * H], F32R)
        mixed_pick = sb("mixed_pick", [KR, H, P], F32R)
        iota_part = sb("iota_part", [P, 1])
        iota_row = sb("iota_row", [P, SYM], BF16)
        iota_code = sb("iota_code", [P, B * STATES])
        hot_id = sb("hot_id", [P, NT])
        head_mask = sb("head_mask", [P, H])
        batch_sel = sb("batch_sel", [B * STATES, 3, B, H], BF16)
        state_absent = sb("state_absent", [B * STATES, STATES])
        before = sb("before", [P, E, E])
        neg_half = sb("neg_half", [P, NT])
        warm = sb("warm", [P, 1])
        warm2 = sb("warm2", [P, 1])

        x_f = sb("x_f", [P, B, J])
        x_b = sb("x_b", [P, B * J], BF16)
        ends_f = sb("ends_f", [P, 2])
        code0 = sb("code0", [P, B, J])
        code = sb("code", [P, B, J])
        no_end = sb("no_end", [P, B, J])
        local = sb("local", [P, B, J])
        final = sb("final", [P, B, J])
        state = sb("state", [P, B, J])
        cls = sb("cls", [P, B, J])
        hot_code = sb("hot_code", [P, B * J, B * STATES], BF16)
        total_row = sb("total_row", [B, P])
        total_none = sb("total_none", [B, P])
        carry_row = sb("carry_row", [B, P + 1])
        carry = sb("carry", [P, B])
        count_row = sb("count_row", [B * STATES, SYM])
        is_absent = sb("is_absent", [B * STATES, SYM])
        penalty = sb("penalty", [B * STATES, STATES, SYM], BF16)
        count = sb("count", [P, B * STATES])
        cls_row = sb("cls_row", [B * J, P], BF16)
        hot = sb("hot", [P, NT, J, P], F32R)

        end_hot = sb("end_hot", [SYM, 4])
        gather = sb("gather", [SYM, 4, SYM])
        stats = sb("stats", [P, NT, 6])
        mv = sb("mv", [P, NT, 2])
        var = sb("var", [P, 2, NT])
        rstd = sb("rstd", [P, 2, NT])
        xn = sb("xn", [P, 2, D])
        xn_t = sb("xn_t", [P, 2 * P])
        h0 = sb("h0", [P, NT, D])
        u_h0 = sb("u_h0", [P, NT, D])
        q_cols = sb("q_cols", [P, H])
        k_cols = sb("k_cols", [P, 3, B, H])
        keys_hl = sb("keys_hl", [KR, CLS], F32R)
        neg_q = sb("neg_q", [P, NT, H])
        v_aug = sb("v_aug", [P, STATES, PAIRS, 2, HA])
        v_cnt = sb("v_cnt", [P, B, STATES, PAIRS, HALF])
        RING = 4
        dist = sb("dist", [P, RING, STATES, 2, SYM])
        iota_sym = (dist[:].rearrange("p r s m c -> p (r s m c)")[:, 0:SYM * B * J // 2].bitcast(BF16)
                    .rearrange("p (c t) -> p c t", c=SYM))
        near = sb("near", [P, UNITS, 2])
        shift = sb("shift", [P, UNITS, 2])
        prob_t = sb("prob_t", [P, RING, STATES, P])
        hot_sym = (prob_t[:].rearrange("p r s q -> p (r s q)")[:, 0:SYM * B * J // 2].bitcast(BF16)
                   .rearrange("p (c t) -> p c t", c=SYM))
        rden = sb("rden", [P, NT, PAIRS, 2])
        o_sb = sb("o_sb", [P, 2, 2 * P])
        heads = sb("heads", [P, NT, PAIRS, 2, HD])
        heads_t = sb("heads_t", [P, NT, P])
        h1 = sb("h1", [P, NT, D])
        stats3 = sb("stats3", [P, NT, 6])
        mv3 = sb("mv3", [P, NT, 2])
        var3 = sb("var3", [P, NT, 2])
        rstd3 = sb("rstd3", [P, NT, 2])
        hn = sb("hn", [P, NT, D])
        hn_t = sb("hn_t", [P, ROWS])
        hn_hi = sb("hn_hi", [P, ROWS], F32R)
        hn_lo = sb("hn_lo", [P, ROWS], F32R)

        logit = sb("logit", [P, NT, E])
        above = sb("above", [P, NT, E, E])
        tie = sb("tie", [P, NT, E, E])
        rank = sb("rank", [P, NT, E])
        top = sb("top", [P, NT, 1])
        shifted = sb("shifted", [P, NT, E])
        e_exp = sb("e_exp", [P, NT, E])
        chosen = sb("chosen", [P, NT, E])
        gsum = sb("gsum", [P, NT, 1])
        grec = sb("grec", [P, NT, 1])
        gate = sb("gate", [P, NT, GR // E, E])
        gates_hl = sb("gates_hl", [GR, ROWS], F32R)

        hid_hi = sb("hid_hi", [P, 2, FT, ROWS], F32R)
        hid_lo = sb("hid_lo", [P, 2, FT, ROWS], F32R)
        w1_flat = w1_f[:].rearrange("p e f -> p (e f)")
        hid = w1_flat[:, 0:2 * FT * ROWS].rearrange("p (k t r) -> p k t r", k=2, t=FT)
        base = w1_flat[:, 2 * FT * ROWS:2 * FT * ROWS + ROWS].rearrange("p (t d) -> p t d", t=NT)
        w_ln = w1_flat[:, 2 * FT * ROWS + ROWS:2 * FT * ROWS + 2 * ROWS].rearrange("p (t d) -> p t d", t=NT)
        w2_flat = w2_f[:].rearrange("p e t d -> p (e t d)")
        term = w2_flat[:, 0:2 * ROWS].rearrange("p (k r) -> p k r", k=2)
        acc = w2_flat[:, 2 * ROWS:3 * ROWS]
        gate_bc = w2_flat[:, 4 * ROWS:6 * ROWS].rearrange("p (k r) -> p k r", k=2)
        tab = sb("tab", [P, NT, 2, D], F32R)
        y = w1_f[:].rearrange("p e (j d) -> p (e j) d", d=D).rearrange("p (b j) d -> p b j d", b=B)

        x_in = sem("x_in")
        end_in = sem("end_in")
        emb_in = sem("emb_in")
        cols_in = sem("cols_in")
        wv_in = sem("wv_in")
        small_in = sem("small_in")
        w1_in = [sem(f"w1_in{i}") for i in range(4)]
        w2_in = [sem(f"w2_in{i}") for i in range(4)]
        y_out = sem("y_out")
        pool_step = sem("pool_step")
        ident_ready = sem("ident_ready")
        mask_ready = sem("mask_ready")
        iota_ready = sem("iota_ready")
        select_ready = sem("select_ready")
        diag_ready = sem("diag_ready")
        aug_zero = sem("aug_zero")
        small_ident = sem("small_ident")
        mixed_ready = sem("mixed_ready")
        gather_ready = sem("gather_ready")
        h0_done = sem("h0_done")
        h0_ready = sem("h0_ready")
        var_ready = sem("var_ready")
        rstd_ready = sem("rstd_ready")
        var3_ready = sem("var3_ready")
        rstd3_ready = sem("rstd3_ready")
        xn_ready = sem("xn_ready")
        xnt_done = sem("xnt_done")
        xnt_ready = sem("xnt_ready")
        qk_cols = sem("qk_cols")
        q_done = sem("q_done")
        v_done = sem("v_done")
        negq_ready = sem("negq_ready")
        total_ready = sem("total_ready")
        total_done = sem("total_done")
        carry_ready = sem("carry_ready")
        carry_done = sem("carry_done")
        hot_ready = sem("hot_ready")
        countrow_done = sem("countrow_done")
        countrow_ready = sem("countrow_ready")
        penalty_ready = sem("penalty_ready")
        keyrow_done = sem("keyrow_done")
        key_split = sem("key_split")
        count_done = sem("count_done")
        count_ready = sem("count_ready")
        cls_ready = sem("cls_ready")
        clsrow_done = sem("clsrow_done")
        clsrow_ready = sem("clsrow_ready")
        v_ready = sem("v_ready")
        kb_done = sem("kb_done")
        dist_ready = sem("dist_ready")
        near_ready = sem("near_ready")
        prob_ready = sem("prob_ready")
        pt_done = sem("pt_done")
        pt_act = sem("pt_act")
        pt_dve = sem("pt_dve")
        o_done = sem("o_done")
        o_taken = sem("o_taken")
        oback_done = sem("oback_done")
        headst_done = sem("headst_done")
        headst_ready = sem("headst_ready")
        heads_ready = sem("heads_ready")
        att_done = sem("att_done")
        att_read = sem("att_read")
        base_ready = sem("base_ready")
        baset_done = sem("baset_done")
        baset_ready = sem("baset_ready")
        hn_ready = sem("hn_ready")
        hnt_done = sem("hnt_done")
        hnt_ready = sem("hnt_ready")
        hn_split = sem("hn_split")
        logit_done = sem("logit_done")
        logit_read = sem("logit_read")
        shifted_ready = sem("shifted_ready")
        gexp_ready = sem("gexp_ready")
        gate_zero = sem("gate_zero")
        gate_ready = sem("gate_ready")
        gatet_done = sem("gatet_done")
        gate_split = sem("gate_split")
        w1_hi_ready = sem("w1_hi_ready")
        w1_lo_ready = sem("w1_lo_ready")
        w2_hi_ready = sem("w2_hi_ready")
        w2_lo_ready = sem("w2_lo_ready")
        up_done = sem("up_done")
        gelu_ready = sem("gelu_ready")
        hi_ready = sem("hi_ready")
        lo_ready = sem("lo_ready")
        down_done = sem("down_done")
        gateb_done = sem("gateb_done")
        gateb_ready = sem("gateb_ready")
        term_ready = sem("term_ready")
        acc_ready = sem("acc_ready")
        bc_done = sem("bc_done")
        hot_out = sem("hot_out")
        mixed_done = sem("mixed_done")
        table_ready = sem("table_ready")
        y_done = sem("y_done")
        y_hi = sem("y_hi")
        y_ready = sem("y_ready")
        dve_step = sem("dve_step")

        BK_H0, BK_XNT, BK_QV, BK_CNT, BK_CHAIN, BK_PT = 4, 5, 6, 7, 3, 4
        O_BANKS = (7, 2)
        ROUTE_BANKS = (3, 4, 5)
        KB = 2
        EARLY_W2 = 5
        QCOL = 2 * P
        TILE_COLS = (slice(0, P), slice(P, 2 * P), slice(HALF, HALF + P))
        PARTS = (((0, 0, P),), ((0, 0, HALF), (1, HALF, P)), ((1, 0, P),))
        HOT_STEPS = NT * J // 4
        Y_GROUPS = B * J // 2
        OUTPUTS = [(0, 1), (1, 1)] + [(g, 2) for g in range(2, Y_GROUPS - 2, 2)] + [(Y_GROUPS - 2, 1), (Y_GROUPS - 1, 1)]
        SMALL = 3

        def by_act(unit):
            return unit in (0, 2, 3, 5, 6, 8, 9, 10)

        def acts_before(unit):
            return len([k for k in range(unit) if by_act(k)])

        def pt_taken(eng, unit):
            if by_act(unit):
                eng.wait_ge(pt_act, acts_before(unit) + 1)
            else:
                eng.wait_ge(pt_dve, unit - acts_before(unit) + 1)

        block = ctx.enter_context(nc.Block())

        @block.sync
        def _(sp):
            sp.dma_start(x_i[:], x.rearrange("b (p j) -> p b j", p=P)).then_inc(x_in, 16)
            sp.dma_start(emb[:], weight).then_inc(emb_in, 16)
            sp.dma_start(wv_rows[:], wv).then_inc(wv_in, 16)
            for i in range(4):
                sp.dma_start(w1_f[:, 2 * i:2 * i + 2, :],
                             w1[2 * i:2 * i + 2].rearrange("e d f -> d e f")).then_inc(w1_in[i], 16)
            for i in range(4):
                for e in (2 * i, 2 * i + 1):
                    sp.dma_start(w2_f[:, e], w2[e].rearrange("(t f) d -> f t d", f=P)).then_inc(w2_in[i], 16)
            for n, (g, size) in enumerate(OUTPUTS):
                b, j = g * 2 // J, g * 2 % J
                sp.wait_ge(y_ready, g + size)
                sp.dma_start(out[b].rearrange("(p j) d -> p j d", j=J)[:, j:j + 2 * size, :],
                             y[:, b, j:j + 2 * size, :]).then_inc(y_out, 16)
            sp.wait_ge(y_out, 16 * len(OUTPUTS))

        @block.gpsimd
        def _(pool):
            n = 0

            def step(ins):
                nonlocal n
                n += 1
                ins.then_inc(pool_step, 1)

            def settle():
                pool.wait_ge(pool_step, n)

            G = nc.gpsimd
            step(G.memset(ident[:], 0.0))
            step(G.memset(head_mask[:], 1.0))
            settle()
            G.affine_select(out=ident[:], in_=ident[:], compare_op=ALU.not_equal, fill=1.0,
                            base=0, pattern=[[-1, P]], channel_multiplier=1).then_inc(ident_ready, 1)
            G.iota(iota_part[:], pattern=[[0, 1]], base=0, channel_multiplier=1,
                   allow_small_or_imprecise_dtypes=True).then_inc(ident_ready, 1)
            G.iota(iota_row[:], pattern=[[1, SYM]], base=0, channel_multiplier=0,
                   allow_small_or_imprecise_dtypes=True).then_inc(iota_ready, 1)
            step(G.affine_select(out=head_mask[:], in_=head_mask[:], compare_op=ALU.is_ge, fill=0.0,
                                 base=0, pattern=[[-HD, H]], channel_multiplier=1))
            settle()
            G.affine_select(out=head_mask[:], in_=head_mask[:], compare_op=ALU.is_ge, fill=0.0,
                            base=HD - 1, pattern=[[HD, H]], channel_multiplier=-1).then_inc(mask_ready, 1)
            G.iota(iota_code[:], pattern=[[1, B * STATES]], base=0, channel_multiplier=0,
                   allow_small_or_imprecise_dtypes=True).then_inc(iota_ready, 1)
            step(G.memset(neg_half[:], -0.5))
            step(G.memset(batch_sel[:, 0], 1.0))
            step(G.memset(batch_sel[:, 1], 0.0))
            step(G.memset(batch_sel[:, 2], 1.0))
            step(G.memset(state_absent[:], 0.0))
            step(G.memset(before[:], 1.0))
            settle()
            step(G.affine_select(out=batch_sel[:, :, 0], in_=batch_sel[:, :, 0], compare_op=ALU.is_ge, fill=0.0,
                                 base=STATES - 1, pattern=[[0, 3], [0, H]], channel_multiplier=-1))
            step(G.affine_select(out=batch_sel[:, :, 1], in_=batch_sel[:, :, 1], compare_op=ALU.is_ge, fill=0.0,
                                 base=-STATES, pattern=[[0, 3], [0, H]], channel_multiplier=1))
            for b in range(B):
                step(G.affine_select(out=state_absent[:], in_=state_absent[:], compare_op=ALU.not_equal,
                                     fill=ABSENT, base=-STATES * b, pattern=[[-1, STATES]],
                                     channel_multiplier=1))
                settle()
            G.affine_select(out=before[:], in_=before[:], compare_op=ALU.is_gt, fill=0.0, base=0,
                            pattern=[[1, E], [-1, E]], channel_multiplier=0).then_inc(select_ready, 1)
            G.memset(v_aug[:], 0.0).then_inc(aug_zero, 1)
            G.memset(v_cnt[:], 0.0).then_inc(aug_zero, 1)
            G.memset(gate[:], 0.0).then_inc(gate_zero, 1)
            pool.wait_ge(var_ready, 1)
            G.tensor_tensor(rstd[:, 1, 0:2], var[:, 1, 0:2], neg_half[:, 0:2], ALU.pow).then_inc(rstd_ready, 1)

            def low_w1(e):
                pool.wait_ge(w1_hi_ready, e + 1)
                G.tensor_tensor(w1_lo[:, e], w1_f[:, e], w1_hi[:, e].bitcast(F32), ALU.subtract).then_inc(w1_lo_ready, 1)

            def low_w2(e):
                pool.wait_ge(w2_hi_ready, e + 1)
                G.tensor_tensor(w2_lo[:, e], w2_f[:, e], w2_hi[:, e].bitcast(F32), ALU.subtract).then_inc(w2_lo_ready, 1)

            def roots(i):
                for k in (1, 0):
                    pool.wait_ge(var3_ready, 2 * i + 2 - k)
                    G.tensor_tensor(rstd3[:, i, k:k + 1], var3[:, i, k:k + 1], neg_half[:, 0:1],
                                    ALU.pow).then_inc(rstd3_ready, 1)

            low_w1(0)
            pool.wait_ge(var_ready, 2)
            G.tensor_tensor(rstd[:, 0], var[:, 0], neg_half[:], ALU.pow).then_inc(rstd_ready, 1)
            for e in range(1, E):
                low_w1(e)
            roots(0)
            for e in range(2):
                low_w2(e)
            roots(1)
            for e in range(2, EARLY_W2 - 1):
                low_w2(e)
            roots(2)
            low_w2(EARLY_W2 - 1)

            def sum_up(e):
                pool.wait_ge(term_ready, e + 1)
                if e == 0:
                    pool.wait_ge(baset_ready, 1)
                else:
                    pool.wait_ge(acc_ready, e)
                G.tensor_tensor(acc, acc, term[:, e % 2], ALU.add).then_inc(acc_ready, 1)

            for e in range(E):
                for f in range(FT):
                    pool.wait_ge(gelu_ready, e * FT + f + 1)
                    if e >= 2:
                        pool.wait_ge(down_done, FT * (e - 2) + f + 1)
                    G.tensor_scalar(hid_hi[:, e % 2, f], hid[:, e % 2, f], 1.0, 0.0,
                                    ALU.mult, ALU.add).then_inc(hi_ready, 1)
                    if e >= 3 and f == 0:
                        sum_up(e - 3)
                if e < E - EARLY_W2:
                    low_w2(e + EARLY_W2)
            sum_up(E - 3)

        @block.scalar
        def _(act):
            act.dma_start(ends_i[:], end_ids.to_broadcast([P, 2])).then_inc(end_in, 16)
            act.dma_start(cols[:], columns).then_inc(cols_in, 16)
            for dst, src in ((wm_sb[:], wm), (br_row[:], b_r.to_broadcast([P, E])), (ffn_cols[:], ffn_columns)):
                act.dma_start(dst, src).then_inc(small_in, 16)
            act.wait_ge(ident_ready, 2)
            nc.scalar.activation(warm[:], iota_part[:], ACT.Exp, scale=-1.0)
            act.wait_ge(h0_done, 1)
            nc.scalar.activation(h0[:], ps[:, BK_H0, 0:NT * D].rearrange("p (t d) -> p t d", t=NT),
                                 ACT.Copy).then_inc(h0_ready, 1)

            def high_w1(e):
                act.wait_ge(w1_in[e // 2], 16)
                nc.scalar.activation(w1_hi[:, e], w1_f[:, e], ACT.Copy).then_inc(w1_hi_ready, 1)

            def high_w2(e):
                act.wait_ge(w2_in[e // 2], 32)
                nc.scalar.activation(w2_hi[:, e], w2_f[:, e], ACT.Copy).then_inc(w2_hi_ready, 1)

            def squares(unit):
                i, k = unit // PAIRS, unit % PAIRS
                act.wait_ge(kb_done, unit + 1)
                if unit >= RING:
                    act.wait_ge(pt_done, unit - RING + 1)
                for m in range(2):
                    h = 2 * k + m
                    nc.scalar.activation(dist[:, unit % RING, :, m],
                                         ps[:, unit % KB, m * CLS:(m + 1) * CLS].rearrange("p (s c) -> p s c", s=STATES),
                                         ACT.Square, bias=neg_q[:, i, h:h + 1]).then_inc(dist_ready, 1)

            def exps(unit):
                act.wait_ge(near_ready, unit + 1)
                for m in range(2):
                    d = dist[:, unit % RING, :, m]
                    nc.scalar.activation(d, d, ACT.Exp, scale=-1.0 / HD ** 0.5,
                                         bias=shift[:, unit, m:m + 1]).then_inc(prob_ready, 1)

            def take(unit):
                if by_act(unit):
                    act.wait_ge(pt_done, unit + 1)
                    if unit >= RING:
                        act.wait_ge(o_done, unit - RING + 1)
                    nc.scalar.activation(prob_t[:, unit % RING], ps[:, BK_PT + unit % 3, 0:STATES * P]
                                         .rearrange("p (s q) -> p s q", s=STATES), ACT.Copy).then_inc(pt_act, 1)

            for e in range(E):
                high_w1(e)
            act.wait_ge(negq_ready, 1)
            squares(0)
            squares(1)
            for unit in range(UNITS):
                if unit + 2 < UNITS:
                    squares(unit + 2)
                exps(unit)
                if unit >= 1:
                    take(unit - 1)
                if unit >= 4 and unit < 4 + EARLY_W2:
                    high_w2(unit - 4)
            take(UNITS - 1)
            act.wait_ge(shifted_ready, 1)
            nc.scalar.activation(e_exp[:], shifted[:], ACT.Exp).then_inc(gexp_ready, 1)
            nc.scalar.activation(warm2[:], iota_part[:], ACT.Gelu)
            act.wait_ge(small_in, 16 * SMALL)

            def take_gates(e):
                act.wait_ge(gateb_done, e + 1)
                if e >= 2:
                    act.wait_ge(term_ready, e - 1)
                nc.scalar.activation(gate_bc[:, e % 2], ps[:, 6, 0:ROWS], ACT.Copy).then_inc(gateb_ready, 1)

            for e in range(E):
                for f in range(FT):
                    n = e * FT + f
                    act.wait_ge(up_done, n + 1)
                    if e >= 2:
                        act.wait_ge(hi_ready, n - 2 * FT + 1)
                        act.wait_ge(lo_ready, n - 2 * FT + 1)
                    nc.scalar.activation(hid[:, e % 2, f], ps[:, n % 4, 0:ROWS], ACT.Gelu,
                                         bias=b1_col[:, e, f:f + 1]).then_inc(gelu_ready, 1)
                    if e == 2 and f == 0:
                        act.wait_ge(baset_done, 1)
                        nc.scalar.activation(acc, ps[:, 6, 0:ROWS], ACT.Copy).then_inc(baset_ready, 1)
                    if e >= 2 and f == (2 if e == 2 else 1):
                        take_gates(e - 2)
                if e < E - EARLY_W2:
                    high_w2(e + EARLY_W2)
            take_gates(E - 2)
            take_gates(E - 1)
            for g in range(Y_GROUPS):
                act.wait_ge(y_done, g + 1)
                nc.scalar.activation(y[:, g * 2 // J, g * 2 % J:g * 2 % J + 2],
                                     ps[:, (g + NT) % 8, :].rearrange("p (j k d) -> p j k d", j=2, k=2)[:, :, 0],
                                     ACT.Copy).then_inc(y_hi, 1)

        @block.vector
        def _(dve):
            n = 0

            def step(ins):
                nonlocal n
                n += 1
                ins.then_inc(dve_step, 1)

            def settle():
                dve.wait_ge(dve_step, n)

            V = nc.vector
            dve.wait_ge(iota_ready, 1)
            step(V.tensor_copy(iota_sym, iota_row[:].unsqueeze(2).to_broadcast([P, SYM, B * J])))
            step(V.memset(end_hot[:], 0.0))
            step(V.memset(carry_row[:, P:P + 1], 0.0))
            dve.wait_ge(end_in, 16)
            step(V.tensor_copy(ends_f[:], ends_i[:]))
            dve.wait_ge(ident_ready, 2)
            settle()
            for s, k in ((1, 1), (2, 0)):
                step(V.tensor_scalar(end_hot[:, s:s + 1], iota_part[0:SYM], ends_f[0:SYM, k:k + 1], 1.5,
                                     ALU.is_equal, ALU.mult))
            dve.wait_ge(x_in, 16)
            step(V.tensor_copy(x_f[:], x_i[:]))
            settle()
            blocks = [SYM, 4, SYM]
            V.tensor_tensor(gather[:], ident[0:SYM, 0:SYM].unsqueeze(1).to_broadcast(blocks),
                            end_hot[:].unsqueeze(2).to_broadcast(blocks), ALU.add).then_inc(gather_ready, 1)

            step(V.tensor_scalar(code0[:], x_f[:], ends_f[:, 0:1], 2.0, ALU.is_equal, ALU.mult))
            settle()
            step(V.scalar_tensor_tensor(out=code[:], in0=x_f[:], scalar=ends_f[:, 1:2], in1=code0[:],
                                        op0=ALU.is_equal, op1=ALU.max))
            settle()
            step(V.tensor_scalar(no_end[:], code[:], 0.0, None, ALU.is_equal))
            settle()
            for b in range(B):
                V.tensor_tensor_scan(local[:, b, ::-1], no_end[:, b, ::-1], code[:, b, ::-1], 0.0,
                                     ALU.mult, ALU.add).then_inc(total_ready, 1)
            step(V.tensor_copy(x_b[:], x_f[:].rearrange("p b j -> p (b j)")))
            dve.wait_ge(total_done, 1)
            step(V.tensor_copy(total_row[:], ps[0:B, BK_CNT, 0:P]))
            settle()
            step(V.tensor_scalar(total_none[:], total_row[:], 0.0, None, ALU.is_equal))
            settle()
            V.tensor_tensor_scan(carry_row[:, 0:P][:, ::-1], total_none[:, ::-1], total_row[:, ::-1], 0.0,
                                 ALU.mult, ALU.add).then_inc(carry_ready, 1)

            def moments(src, i, st, m):
                step(V.bn_stats(st[:, i], src))
                settle()
                step(V.bn_aggr(m[:, i], st[:, i]))
                settle()

            dve.wait_ge(carry_done, 1)
            step(V.tensor_copy(carry[:], ps[:, BK_CNT, P:P + B]))
            settle()
            for b in range(B):
                step(V.tensor_tensor_scan(final[:, b, ::-1], no_end[:, b, ::-1], code[:, b, ::-1],
                                          carry[:, b:b + 1], ALU.mult, ALU.add))
            settle()
            step(V.tensor_tensor(state[:], final[:], no_end[:], ALU.mult))
            dve.wait_ge(h0_ready, 1)
            for i in range(2):
                step(V.bn_stats(stats[:, i], h0[:, i]))
            settle()
            for i in range(2):
                step(V.bn_aggr(mv[:, i], stats[:, i]))
            V.scalar_tensor_tensor(out=cls[:], in0=state[:], scalar=float(SYM), in1=x_f[:], op0=ALU.mult,
                                   op1=ALU.add).then_inc(cls_ready, 1)
            settle()
            V.tensor_scalar(var[:, 1, 0:2], mv[:, 0:2, 1], 1.0 + EPS, EPS * EPS, ALU.mult, ALU.add).then_inc(var_ready, 1)
            dve.wait_ge(cls_ready, 1)
            step(V.tensor_scalar(state[:, 1], state[:, 1], float(STATES), None, ALU.add))
            settle()
            dve.wait_ge(iota_ready, 2)
            codes = [P, B * J, B * STATES]
            V.tensor_tensor(hot_code[:], state[:].rearrange("p b j -> p (b j)").unsqueeze(2).to_broadcast(codes),
                            iota_code[:].unsqueeze(1).to_broadcast(codes), ALU.is_equal).then_inc(hot_ready, 1)

            def hot_symbols(b):
                half = slice(b * J, (b + 1) * J)
                V.tensor_tensor(hot_sym[:, :, half], x_b[:, half].unsqueeze(1).to_broadcast([P, SYM, J]),
                                iota_sym[:, :, half], ALU.is_equal).then_inc(hot_ready, 1)

            hot_symbols(0)
            dve.wait_ge(rstd_ready, 1)
            for i in range(2):
                V.tensor_scalar(xn[:, i], h0[:, i], mv[:, i, 0:1], rstd[:, 1, i:i + 1], ALU.subtract,
                                ALU.mult).then_inc(xn_ready, 1)
            hot_symbols(1)
            dve.wait_ge(cols_in, 16)
            dve.wait_ge(mask_ready, 1)
            V.tensor_scalar(q_cols[:], head_mask[:], wq_col, None, ALU.mult).then_inc(qk_cols, 1)
            V.memset(k_cols[:, 1], 0.0).then_inc(qk_cols, 1)
            for g in (0, 2):
                V.tensor_scalar(k_cols[:, g], head_mask[:].unsqueeze(1).to_broadcast([P, B, H]), wk_col,
                                None, ALU.mult).then_inc(qk_cols, 1)
            dve.wait_ge(wv_in, 16)
            V.tensor_tensor(wv_diag[:].rearrange("p (h e) -> p h e", h=H), wv_rows[:].unsqueeze(1).to_broadcast([P, H, HD]),
                            head_mask[:].unsqueeze(2).to_broadcast([P, H, HD]), ALU.mult).then_inc(diag_ready, 1)
            dve.wait_ge(xnt_done, 1)
            V.tensor_copy(xn_t[:], ps[:, BK_XNT, 0:2 * P]).then_inc(xnt_ready, 1)
            V.tensor_copy(pick[0:LOW], ident[0:LOW, 0:B * H]).then_inc(small_ident, 1)
            V.tensor_copy(pick[LOW:KR], ident[LOW:KR, LOW:KR]).then_inc(small_ident, 1)
            dve.wait_ge(select_ready, 1)
            dve.wait_ge(countrow_done, 1)
            V.tensor_copy(count_row[:], ps[0:B * STATES, BK_CNT, 192:192 + SYM]).then_inc(countrow_ready, 1)
            dve.wait_ge(countrow_ready, 1)
            step(V.tensor_scalar(is_absent[:], count_row[:], 0.0, None, ALU.is_equal))
            settle()
            pens = [B * STATES, STATES, SYM]
            V.tensor_tensor(penalty[:], is_absent[:].unsqueeze(1).to_broadcast(pens),
                            state_absent[:].unsqueeze(2).to_broadcast(pens), ALU.mult).then_inc(penalty_ready, 1)
            dve.wait_ge(keyrow_done, 1)
            V.tensor_copy(keys_hl[:], ps[0:KR, BK_CHAIN, 0:CLS]).then_inc(key_split, 1)
            dve.wait_ge(key_split, 1)
            V.tensor_tensor(keys_hl[LOW:KR], ps[LOW:KR, BK_CHAIN, 0:CLS], keys_hl[LOW:KR].bitcast(F32),
                            ALU.subtract).then_inc(key_split, 1)
            dve.wait_ge(q_done, 1)
            V.tensor_scalar(neg_q[:].rearrange("p t h -> p (t h)"), ps[:, BK_XNT, QCOL:QCOL + NT * H], -1.0, None,
                            ALU.mult).then_inc(negq_ready, 1)
            dve.wait_ge(count_done, 1)
            V.tensor_copy(count[:], ps[:, BK_CNT, 256:256 + B * STATES]).then_inc(count_ready, 1)

            def values_in():
                dve.wait_ge(aug_zero, 2)
                for par in range(2):
                    half = slice(par * HALF, (par + 1) * HALF)
                    dve.wait_ge(v_done, par + 1)
                    step(V.memset(v_aug[half, :, :, par, HD:HA], 1.0))
                    for st in range(STATES):
                        step(V.tensor_copy(v_aug[half, st, :, par, 0:HD],
                                           ps[half, BK_QV, st * D:(st + 1) * D]
                                           .rearrange("p (k m e) -> p k m e", k=PAIRS, m=2)[:, :, par]))

            def pick_by_batch():
                for a, z, c in ((0, LOW, 0), (LOW, KR, LOW)):
                    V.tensor_copy(mixed_pick[a:z].rearrange("k h (b p) -> k b h p", b=B),
                                  ident[a:z, c:c + B * H].rearrange("k (b h) -> k b h", b=B).unsqueeze(3)
                                  .to_broadcast([z - a, B, H, HALF])).then_inc(mixed_ready, 1)
                V.tensor_copy(ident_b[:], ident[0:B * J, 0:B * J]).then_inc(mixed_ready, 1)

            def weigh_values(b):
                if b == 0:
                    dve.wait_ge(count_ready, 1)
                    settle()
                for st in range(STATES):
                    c = b * STATES + st
                    V.tensor_scalar(v_cnt[:, b, st, :, 0:2 * HA], v_aug[:, st].rearrange("p k m e -> p k (m e)"),
                                    count[:, c:c + 1], None, ALU.mult).then_inc(v_ready, 1)
                if b == 0:
                    dve.wait_ge(clsrow_done, 1)
                    V.tensor_copy(cls_row[:], ps[0:B * J, BK_CNT, 384:512]).then_inc(clsrow_ready, 1)

            def rest_of_rows():
                step(V.bn_stats(stats[:, 2], h0[:, 2]))
                settle()
                step(V.bn_aggr(mv[:, 2], stats[:, 2]))
                settle()
                V.tensor_scalar(var[:, 0], mv[:, :, 1], EPS, None, ALU.add).then_inc(var_ready, 1)
                for t, a, z, first in ((0, 0, P, 0), (1, 0, HALF, P), (1, HALF, P, -HALF), (2, 0, P, HALF)):
                    step(V.tensor_scalar(hot_id[a:z, t:t + 1], iota_part[a:z], float(first), None, ALU.add))

            def residual_base(i):
                if i == 0:
                    dve.wait_ge(rstd_ready, 2)
                step(V.tensor_scalar(u_h0[:, i], h0[:, i], mv[:, i, 0:1], rstd[:, 0, i:i + 1], ALU.subtract, ALU.mult))
                settle()
                step(V.tensor_tensor(u_h0[:, i], u_h0[:, i], h0[:, i], ALU.add))

            def nearest(unit):
                dve.wait_ge(dist_ready, 2 * (unit + 1))
                step(V.tensor_reduce(near[:, unit], dist[:, unit % RING].rearrange("p s m c -> p m s c"), AX.XY, ALU.min))
                settle()
                V.tensor_scalar(shift[:, unit], near[:, unit], 1.0 / HD ** 0.5, None, ALU.mult).then_inc(near_ready, 1)

            def take(unit):
                if not by_act(unit):
                    dve.wait_ge(pt_done, unit + 1)
                    if unit >= RING:
                        dve.wait_ge(o_done, unit - RING + 1)
                    V.tensor_copy(prob_t[:, unit % RING], ps[:, BK_PT + unit % 3, 0:STATES * P]
                                  .rearrange("p (s q) -> p s q", s=STATES)).then_inc(pt_dve, 1)

            def take_values(i):
                dve.wait_ge(o_done, PAIRS * (i + 1))
                V.tensor_copy(o_sb[:, i % 2], ps[:, O_BANKS[i % 2], 0:2 * P]).then_inc(o_taken, 1)

            def normalise_heads(i):
                dve.wait_ge(oback_done, i + 1)
                o = (ps[:, BK_CHAIN, 0:2 * P].rearrange("p (k c) -> p k c", k=PAIRS)[:, :, 0:2 * HA]
                     .rearrange("p k (m e) -> p k m e", m=2))
                step(V.reciprocal(rden[:, i], o[:, :, :, HD]))
                settle()
                V.tensor_tensor(heads[:, i], o[:, :, :, 0:HD], rden[:, i].unsqueeze(3).to_broadcast([P, PAIRS, 2, HD]),
                                ALU.mult).then_inc(heads_ready, 1)

            def turn_heads(i):
                dve.wait_ge(headst_done, i + 1)
                V.tensor_copy(heads_t[:, i], ps[:, BK_CHAIN, 2 * P:3 * P]).then_inc(headst_ready, 1)

            def residual(i):
                dve.wait_ge(att_done, i + 1)
                V.tensor_tensor(h1[:, i], ps[:, BK_CHAIN, 3 * P:4 * P], u_h0[:, i], ALU.add).then_inc(att_read, 1)
                dve.wait_ge(att_read, i + 1)
                moments(h1[:, i], i, stats3, mv3)
                V.tensor_scalar(var3[:, i, 1:2], mv3[:, i, 1:2], 1.0 + EPS, EPS * EPS, ALU.mult, ALU.add).then_inc(var3_ready, 1)
                V.tensor_scalar(var3[:, i, 0:1], mv3[:, i, 1:2], EPS, None, ALU.add).then_inc(var3_ready, 1)

            def double_norm(i):
                dve.wait_ge(rstd3_ready, 2 * i + 1)
                V.tensor_scalar(hn[:, i], h1[:, i], mv3[:, i, 0:1], rstd3[:, i, 1:2], ALU.subtract, ALU.mult).then_inc(hn_ready, 1)

            def take_rows(i):
                c = slice(i * P, (i + 1) * P)
                dve.wait_ge(hnt_done, i + 1)
                V.tensor_scalar(hn_t[:, c], ps[:, ROUTE_BANKS[i], 0:P], g_col, b_col, ALU.mult,
                                ALU.add).then_inc(hnt_ready, 1)

            def split_rows(i):
                c = slice(i * P, (i + 1) * P)
                dve.wait_ge(hnt_ready, i + 1)
                V.tensor_copy(hn_hi[:, c], hn_t[:, c]).then_inc(hn_split, 1)
                dve.wait_ge(hn_split, 2 * i + 1)
                V.tensor_tensor(hn_lo[:, c], hn_t[:, c], hn_hi[:, c].bitcast(F32), ALU.subtract).then_inc(hn_split, 1)

            def read_logits(i):
                dve.wait_ge(logit_done, i + 1)
                V.tensor_tensor(logit[:, i], ps[:, ROUTE_BANKS[i], P:P + E], br_row[:], ALU.add).then_inc(logit_read, 1)

            def base_rows(i):
                dve.wait_ge(rstd3_ready, 2 * i + 2)
                step(V.tensor_scalar(w_ln[:, i], h1[:, i], mv3[:, i, 0:1], rstd3[:, i, 0:1], ALU.subtract, ALU.mult))
                settle()
                V.tensor_tensor(base[:, i], h1[:, i], w_ln[:, i], ALU.add).then_inc(base_ready, 1)

            pick_by_batch()
            dve.wait_ge(small_in, 16 * SMALL)
            for unit in range(UNITS):
                i, k = unit // PAIRS - 1, unit % PAIRS
                if unit != 1:
                    nearest(unit)
                if i >= 0 and k == 2:
                    normalise_heads(i)
                if i >= 0 and k == 3:
                    residual(i)
                if unit == 9:
                    take_rows(0)
                    split_rows(0)
                if unit >= 1:
                    take(unit - 1)
                if unit == 0:
                    nearest(1)
                    values_in()
                    weigh_values(0)
                if unit == 2:
                    weigh_values(1)
                    rest_of_rows()
                if 3 <= unit < 3 + NT:
                    residual_base(unit - 3)
                if i >= 0 and k == 1:
                    take_values(i)
                if i >= 0 and k == 2:
                    turn_heads(i)
                if i >= 0 and k == 3:
                    double_norm(i)
                if unit == 8:
                    base_rows(0)
                if unit == 9:
                    read_logits(0)
            take(UNITS - 1)
            take_values(2)
            normalise_heads(2)
            take_rows(1)
            turn_heads(2)
            split_rows(1)
            residual(2)
            read_logits(1)
            base_rows(1)
            double_norm(2)
            take_rows(2)
            split_rows(2)
            read_logits(2)

            dve.wait_ge(logit_read, NT)
            step(V.tensor_reduce(top[:, :, 0], logit[:], AX.X, ALU.max))
            settle()
            V.tensor_tensor(shifted[:], logit[:], top[:].to_broadcast([P, NT, E]), ALU.subtract).then_inc(shifted_ready, 1)
            pairs = [P, NT, E, E]
            other = logit[:].unsqueeze(2).to_broadcast(pairs)
            own = logit[:].unsqueeze(3).to_broadcast(pairs)
            step(V.tensor_tensor(tie[:], other, own, ALU.is_equal))
            step(V.tensor_tensor(above[:], other, own, ALU.is_gt))
            settle()
            step(V.tensor_tensor(tie[:], tie[:], before[:].unsqueeze(1).to_broadcast(pairs), ALU.mult))
            settle()
            step(V.tensor_tensor(above[:], above[:], tie[:], ALU.add))
            settle()
            step(V.tensor_reduce(rank[:], above[:], AX.X, ALU.add))
            settle()
            dve.wait_ge(gexp_ready, 1)
            step(V.scalar_tensor_tensor(out=chosen[:], in0=rank[:], scalar=2.0, in1=e_exp[:], op0=ALU.is_lt,
                                        op1=ALU.mult))
            settle()
            step(V.tensor_reduce(gsum[:, :, 0], chosen[:], AX.X, ALU.add))
            settle()
            step(V.reciprocal(grec[:], gsum[:]))
            settle()
            dve.wait_ge(gate_zero, 1)
            twice = [P, NT, 2, E]
            V.tensor_tensor(gate[:, :, 0:GR // E:LOW // E], chosen[:].unsqueeze(2).to_broadcast(twice),
                            grec[:].unsqueeze(3).to_broadcast(twice), ALU.mult).then_inc(gate_ready, 1)

            def low_half(e, f):
                k = e * FT + f
                dve.wait_ge(hi_ready, k + 1)
                if e >= 2:
                    dve.wait_ge(down_done, k - 2 * FT + 1)
                V.tensor_tensor(hid_lo[:, e % 2, f], hid[:, e % 2, f], hid_hi[:, e % 2, f].bitcast(F32),
                                ALU.subtract).then_inc(lo_ready, 1)

            def weigh(e, rows=slice(0, ROWS)):
                dve.wait_ge(down_done, FT * (e + 1))
                dve.wait_ge(gateb_ready, e + 1)
                if e >= 2:
                    dve.wait_ge(acc_ready, e - 1)
                V.scalar_tensor_tensor(out=term[:, e % 2, rows], in0=ps[:, 4 + e % 2, rows],
                                       scalar=b2_col[:, e:e + 1], in1=gate_bc[:, e % 2, rows],
                                       op0=ALU.add, op1=ALU.mult).then_inc(term_ready, 1)

            def one_hot(g):
                t, j = g // (J // 4), g % (J // 4) * 4
                dve.wait_ge(bc_done, g + 1)
                V.tensor_scalar(hot[:, t, j:j + 4], ps[:, 7, :].rearrange("p (j t) -> p j t", j=4),
                                hot_id[:, t:t + 1], None, ALU.is_equal).then_inc(hot_out, 1)

            for f in range(FT):
                low_half(0, f)
            base_rows(2)
            for e in range(1, E):
                if e < E - 1:
                    one_hot(2 * (e - 1))
                low_half(e, 0)
                low_half(e, 1)
                if e >= 2:
                    weigh(e - 2)
                if e < E - 1:
                    one_hot(2 * e - 1)
                low_half(e, 2)
                if e == 1:
                    dve.wait_ge(gatet_done, NT)
                    V.tensor_copy(gates_hl[:], ps[0:GR, 6, 0:ROWS]).then_inc(gate_split, 1)
                    dve.wait_ge(gate_split, 1)
                    V.tensor_tensor(gates_hl[LOW:GR], ps[LOW:GR, 6, 0:ROWS], gates_hl[LOW:GR].bitcast(F32),
                                    ALU.subtract).then_inc(gate_split, 1)
                low_half(e, 3)
            weigh(E - 2)
            first, last = slice(0, 2 * P), slice(2 * P, ROWS)
            weigh(E - 1, first)
            weigh(E - 1, last)
            for n, (a, z) in enumerate(((0, 2), (2, 3))):
                dve.wait_ge(mixed_done, n + 1)
                V.tensor_copy(tab[:, a:z, 0], ps[:, a:z, 0:D]).then_inc(table_ready, 1)
                dve.wait_ge(table_ready, 2 * n + 1)
                V.tensor_tensor(tab[:, a:z, 1], ps[:, a:z, 0:D], tab[:, a:z, 0].bitcast(F32), ALU.subtract).then_inc(table_ready, 1)
            for g in range(Y_GROUPS):
                dve.wait_ge(y_hi, g + 1)
                dst = y[:, g * 2 // J, g * 2 % J:g * 2 % J + 2]
                V.tensor_tensor(dst, ps[:, (g + NT) % 8, :].rearrange("p (j k d) -> p j k d", j=2, k=2)[:, :, 1], dst,
                                ALU.add).then_inc(y_ready, 1)

        @block.tensor
        def _(pe):
            M = nc.tensor.matmul
            pe.wait_ge(total_ready, B)
            pe.wait_ge(ident_ready, 2)
            nc.tensor.transpose(ps[0:B, BK_CNT, 0:P], local[:, :, 0], ident[:]).then_inc(total_done, 1)
            pe.wait_ge(emb_in, 16)
            pe.wait_ge(gather_ready, 1)
            gathered = gather[:].rearrange("k s c -> k (s c)")
            for i in range(NT):
                if i == NT - 1:
                    pe.wait_ge(carry_ready, 1)
                    nc.tensor.transpose(ps[:, BK_CNT, P:P + B], carry_row[:, 1:P + 1],
                                        ident[0:B, 0:B]).then_inc(carry_done, 1)
                mm = M(ps[:, BK_H0, i * D:(i + 1) * D], gathered[:, TILE_COLS[i]], emb[:], start=True, stop=True)
            mm.then_inc(h0_done, 1)
            for b in range(B):
                pe.wait_ge(hot_ready, 2 + b)
                for k in range(b * J, (b + 1) * J):
                    mm = M(ps[0:B * STATES, BK_CNT, 192:192 + SYM], hot_code[:, k], hot_sym[:, :, k],
                           start=(k == 0), stop=(k == B * J - 1))
                if b == 0:
                    for i in range(2):
                        pe.wait_ge(xn_ready, i + 1)
                        xt = nc.tensor.transpose(ps[:, BK_XNT, i * P:(i + 1) * P], xn[:, i], ident[:])
                    xt.then_inc(xnt_done, 1)
            mm.then_inc(countrow_done, 1)
            pe.wait_ge(xnt_ready, 1)
            pe.wait_ge(qk_cols, 4)
            M(ps[0:KR, BK_CHAIN, 0:CLS], k_cols[:].rearrange("p g b h -> p (g b h)"), xn_t[:, 0:CLS], start=True, stop=False)
            pe.wait_ge(penalty_ready, 1)
            M(ps[0:KR, BK_CHAIN, 0:CLS], batch_sel[:].rearrange("k g b h -> k (g b h)"),
              penalty[:].rearrange("k s c -> k (s c)"), start=False, stop=True).then_inc(keyrow_done, 1)

            for i in range(NT):
                mm = M(ps[:, BK_XNT, QCOL + i * H:QCOL + (i + 1) * H], xn_t[:, TILE_COLS[i]], q_cols[:], start=True, stop=True)
            mm.then_inc(q_done, 1)
            pe.wait_ge(countrow_ready, 1)
            for k in range(2):
                mm = M(ps[k * HALF:(k + 1) * HALF, BK_CNT, 256:256 + B * STATES], count_row[:],
                       ident[0:B * STATES, 0:B * STATES], start=True, stop=True)
            mm.then_inc(count_done, 1)

            def values(par):
                pe.wait_ge(diag_ready, 1)
                for st in range(STATES):
                    mm = M(ps[par * HALF:(par + 1) * HALF, BK_QV, st * D:(st + 1) * D],
                           xn_t[:, st * SYM:(st + 1) * SYM], wv_diag[:], start=True, stop=True)
                mm.then_inc(v_done, 1)

            def keys(unit):
                i, k = unit // PAIRS, unit % PAIRS
                if unit >= KB:
                    pe.wait_ge(dist_ready, 2 * (unit - KB + 1))
                if unit == PAIRS:
                    pe.wait_ge(mixed_ready, 3)
                for m in range(2):
                    h = 2 * k + m
                    row = i // 2 * H + h
                    sel = mixed_pick[:, h] if i == 1 else pick[:, row:row + 1].to_broadcast([KR, P])
                    mm = M(ps[:, unit % KB, m * CLS:(m + 1) * CLS], sel, keys_hl[:], start=True, stop=True)
                mm.then_inc(kb_done, 1)

            def turn_probs(unit):
                pe.wait_ge(prob_ready, 2 * (unit + 1))
                if unit == 2:
                    pe.wait_ge(v_ready, 1)
                if unit >= 3:
                    pt_taken(pe, unit - 3)
                for st in range(STATES):
                    mm = nc.tensor.transpose(ps[:, BK_PT + unit % 3, st * P:(st + 1) * P],
                                             dist[:, unit % RING, st].rearrange("p m c -> p (m c)"), ident[:])
                mm.then_inc(pt_done, 1)

            def weighted(unit):
                i, k = unit // PAIRS, unit % PAIRS
                pt_taken(pe, unit)
                if unit == 0:
                    pe.wait_ge(clsrow_ready, 1)
                pe.wait_ge(v_ready, STATES if i == 0 else B * STATES)
                if k == 0 and i >= 2:
                    pe.wait_ge(o_taken, i - 1)
                base, col = k % 2 * HALF, k // 2 * P
                for b, a, z in PARTS[i]:
                    for st in range(STATES):
                        mm = M(ps[base:base + HALF, O_BANKS[i % 2], col + a:col + z], v_cnt[:, b, st, k],
                               prob_t[:, unit % RING, st, a:z], start=(st == 0), stop=(st == STATES - 1))
                mm.then_inc(o_done, 1)

            def turn_values(i):
                pe.wait_ge(o_taken, i + 1)
                if i == 0:
                    pe.wait_ge(key_split, 2)
                elif i == 1:
                    pe.wait_ge(logit_read, 1)
                else:
                    pe.wait_ge(att_read, i)
                for c in range(2):
                    mm = nc.tensor.transpose(ps[:, BK_CHAIN, c * P:(c + 1) * P], o_sb[:, i % 2, c * P:(c + 1) * P], ident[:])
                mm.then_inc(oback_done, 1)

            def turn_back(i):
                pe.wait_ge(heads_ready, i + 1)
                nc.tensor.transpose(ps[:, BK_CHAIN, 2 * P:3 * P], heads[:, i].rearrange("p k m d -> p (k m d)"),
                                    ident[:]).then_inc(headst_done, 1)

            def output(i):
                pe.wait_ge(headst_ready, i + 1)
                if i == 0:
                    pe.wait_ge(small_in, 16 * SMALL)
                M(ps[:, BK_CHAIN, 3 * P:4 * P], heads_t[:, i], wm_sb[:], start=True, stop=True).then_inc(att_done, 1)

            def turn_rows(i):
                pe.wait_ge(hn_ready, i + 1)
                if i == 0:
                    pe.wait_ge(att_read, 1)
                nc.tensor.transpose(ps[:, ROUTE_BANKS[i], 0:P], hn[:, i], ident[:]).then_inc(hnt_done, 1)

            def route(i):
                pe.wait_ge(hnt_ready, i + 1)
                M(ps[:, ROUTE_BANKS[i], P:P + E], hn_t[:, i * P:(i + 1) * P], wr_t, start=True, stop=True).then_inc(logit_done, 1)

            pe.wait_ge(small_ident, 2)
            pe.wait_ge(key_split, 2)
            keys(0)
            keys(1)
            values(0)
            values(1)
            pe.wait_ge(count_ready, 1)
            nc.tensor.transpose(ps[0:B * J, BK_CNT, 384:512], cls[:].rearrange("p b j -> p (b j)"),
                                ident[:]).then_inc(clsrow_done, 1)
            keys(2)
            for unit in range(UNITS):
                i, k = unit // PAIRS - 1, unit % PAIRS
                if i >= 0 and k == 2:
                    turn_values(i)
                if i >= 0 and k == 3:
                    output(i)
                if unit >= 2:
                    weighted(unit - 2)
                if unit + 3 < UNITS:
                    keys(unit + 3)
                if i >= 0 and k == 2:
                    turn_back(i)
                if unit == 9:
                    route(0)
                turn_probs(unit)
                if unit == 8:
                    turn_rows(0)
            weighted(UNITS - 2)
            weighted(UNITS - 1)
            turn_rows(1)
            turn_values(2)
            turn_back(2)
            route(1)
            output(2)

            def up(e, f, rows=slice(0, ROWS)):
                k = e * FT + f
                pe.wait_ge(w1_lo_ready, e + 1)
                if k >= 4:
                    pe.wait_ge(gelu_ready, k - 3)
                dst = ps[:, k % 4, rows]
                c = slice(f * P, (f + 1) * P)
                M(dst, w1_hi[:, e, c], hn_hi[:, rows], start=True, stop=False)
                M(dst, w1_hi[:, e, c], hn_lo[:, rows], start=False, stop=False)
                return M(dst, w1_lo[:, e, c], hn_hi[:, rows], start=False, stop=True)

            def down(e, f):
                if f == 0:
                    pe.wait_ge(w2_lo_ready, e + 1)
                    if e >= 2:
                        pe.wait_ge(term_ready, e - 1)
                dst = ps[:, 4 + e % 2, 0:ROWS]
                pe.wait_ge(lo_ready, FT * e + f + 1)
                M(dst, w2_hi[:, e, f], hid_hi[:, e % 2, f], start=(f == 0), stop=False)
                M(dst, w2_hi[:, e, f], hid_lo[:, e % 2, f], start=False, stop=False)
                M(dst, w2_lo[:, e, f], hid_hi[:, e % 2, f], start=False, stop=(f == FT - 1)).then_inc(down_done, 1)

            def gates(e):
                if e >= 1:
                    pe.wait_ge(gateb_ready, e)
                else:
                    pe.wait_ge(baset_ready, 1)
                M(ps[:, 6, 0:ROWS], pick[0:GR, e:e + 1].to_broadcast([GR, P]), gates_hl[:], start=True,
                  stop=True).then_inc(gateb_done, 1)

            def class_rows(g):
                t, j0 = g // (J // 4), g % (J // 4) * 4
                if g >= 1:
                    pe.wait_ge(hot_out, g)
                for k in range(4):
                    j = j0 + k
                    if t == 1:
                        for half in range(2):
                            mm = M(ps[half * HALF:(half + 1) * HALF, 7, k * P:(k + 1) * P],
                                   ident_b[:, half * J + j:half * J + j + 1].to_broadcast([B * J, HALF]),
                                   cls_row[:], start=True, stop=True)
                    else:
                        mm = M(ps[:, 7, k * P:(k + 1) * P],
                               ident_b[:, t // 2 * J + j:t // 2 * J + j + 1].to_broadcast([B * J, P]), cls_row[:],
                               start=True, stop=True)
                mm.then_inc(bc_done, 1)

            early_rows, late_rows = slice(0, 2 * P), slice(2 * P, ROWS)
            pe.wait_ge(hn_split, 4)
            pe.wait_ge(dist_ready, 2 * UNITS)
            for f in range(FT - 1):
                up(0, f, early_rows)
            turn_rows(2)
            route(2)
            pe.wait_ge(hn_split, 2 * NT)
            for f in range(FT):
                up(0, f, late_rows if f < FT - 1 else slice(0, ROWS)).then_inc(up_done, 1)

            def turn_base():
                pe.wait_ge(gate_split, 2)
                pe.wait_ge(base_ready, NT)
                for i in range(NT):
                    mm = nc.tensor.transpose(ps[:, 6, i * P:(i + 1) * P], base[:, i], ident[:])
                mm.then_inc(baset_done, 1)

            def turn_gates():
                pe.wait_ge(gate_ready, 1)
                for i in range(NT):
                    nc.tensor.transpose(ps[0:GR, 6, i * P:(i + 1) * P], gate[:, i].rearrange("p g e -> p (g e)"),
                                        ident[:]).then_inc(gatet_done, 1)

            for e in range(1, E):
                for f in range(FT):
                    up(e, f).then_inc(up_done, 1)
                    if e == 1 and f == 1:
                        turn_gates()
                    if f == 0 and e < E - 1:
                        class_rows(2 * (e - 1))
                    if e == 2 and f == 0:
                        turn_base()
                    if e >= 2 and f == (2 if e == 2 else 0):
                        gates(e - 2)
                    if f == 2 and e < E - 1:
                        class_rows(2 * e - 1)
                    if e == E - 1 and f == FT - 1:
                        gates(E - 2)
                    down(e - 1, f)
            for f in range(FT):
                down(E - 1, f)
                if f == 1:
                    gates(E - 1)
            pe.wait_ge(gelu_ready, E * FT)
            for n, tiles in enumerate(((0, 1), (2,))):
                pe.wait_ge(term_ready, E - 1)
                for i in tiles:
                    M(ps[:, i, 0:D], term[:, E % 2, i * P:(i + 1) * P], ident[:], start=True, stop=False)
                pe.wait_ge(acc_ready, E - 2)
                for i in tiles:
                    M(ps[:, i, 0:D], acc[:, i * P:(i + 1) * P], ident[:], start=False, stop=False)
                pe.wait_ge(term_ready, E + n)
                for i in tiles:
                    mm = M(ps[:, i, 0:D], term[:, (E - 1) % 2, i * P:(i + 1) * P], ident[:], start=False, stop=True)
                mm.then_inc(mixed_done, 1)
            pe.wait_ge(hot_out, HOT_STEPS)

            for g in range(Y_GROUPS):
                b, j0 = g * 2 // J, g * 2 % J
                pe.wait_ge(table_ready, 2 if g < 7 else 4)
                if g >= 8:
                    pe.wait_ge(y_ready, g - 7)
                full, part = (0, slice(0, HALF)) if b == 0 else (2, slice(HALF, P))
                for k in range(2):
                    dst = ps[:, (g + NT) % 8, k * 2 * D:(k + 1) * 2 * D]
                    M(dst, hot[:, full, j0 + k], tab[:, full].rearrange("p k d -> p (k d)"), start=True, stop=False)
                    mm = M(dst, hot[part, 1, j0 + k], tab[part, 1].rearrange("p k d -> p (k d)"), start=False, stop=True)
                mm.then_inc(y_done, 1)


def kernel(**inputs):
    import concourse.bacc as bacc
    from concourse.bass_utils import run_bass_kernel_spmd

    pre = {k: np.asarray(v) for k, v in inputs.items()}
    laid = {
        "x": pre["x"],
        "weight": pre["L0_tok_weight"],
        "end_ids": pre["L0_tok_end_ids"].reshape(1, 2),
        "columns": np.stack([pre[k].reshape(P) for k in ("L0_attn_Wq", "L0_attn_Wk", "L0_ffn_ln_g", "L0_ffn_ln_b")], 1),
        "wv": pre["L0_attn_Wv"].reshape(P, HD),
        "wm": pre["L0_attn_Wm"],
        "b_r": pre["L0_ffn_b_r"].reshape(1, E),
        "w1": pre["L0_ffn_W1"],
        "ffn_columns": np.concatenate([pre["L0_ffn_w_r"].T, pre["L0_ffn_b2"].T,
                                       pre["L0_ffn_b1"].reshape(E * FT, P).T], 1),
        "w2": pre["L0_ffn_W2"],
    }
    nc = bacc.Bacc("TRN2", target_bir_lowering=False, num_devices=1)
    arrays, args = {}, []
    for name, a in laid.items():
        a = np.ascontiguousarray(a)
        arrays[f"in_{name}"] = a
        args.append(nc.dram_tensor(f"in_{name}", a.shape, mybir.dt.from_np(a.dtype), kind="ExternalInput").ap())
    args.append(nc.dram_tensor("out_y", (B, T, D), F32, kind="ExternalOutput").ap())
    build(nc, *args)
    r = run_bass_kernel_spmd(nc, [arrays], core_ids=[0])
    return r.results[0]["out_y"]
```
